# Optimizing a Trainium2 kernel written in Bass

```python
import numpy as np
import jax
import jax.numpy as jnp

def _softmax(x, axis=-1):
    return jax.nn.softmax(x, axis=axis)

def _gelu(x):
    return jax.nn.gelu(x, approximate=True)

def _silu(x):
    return jax.nn.silu(x)

def _sigmoid(x):
    return jax.nn.sigmoid(x)

def _layernorm(x, axis=-1, eps=1e-05):
    m = jnp.mean(x, axis=axis, keepdims=True)
    v = jnp.var(x, axis=axis, keepdims=True)
    return (x - m) / jnp.sqrt(v + eps)

def _scatter_add(tgt, idx, src, axis=0):
    return tgt.at[idx].add(src)

def _segment_sum(src, seg, n):
    return jax.ops.segment_sum(src, seg, n)
kernel_name = 'mk_decoder_preln_d1_seqx_r4_33afaa'

def setup_inputs(seed: int=0):
    np.random.seed(seed)
    _w = jnp.asarray

    def _rec_inputs():
        import jax
        import jax.numpy as jnp
        _rk = jax.random.key(seed)
        x = 7.22e-05 + 1 * jax.random.normal(jax.random.fold_in(_rk, 1), (16, 256, 512), jnp.float32)
        _lenS = 256 - jax.random.randint(jax.random.fold_in(_rk, 7), (16,), 0, max(1, 256 // 4) + 1, jnp.int32)
        _lenS2 = 256 - jax.random.randint(jax.random.fold_in(_rk, 8), (16,), 0, max(1, 256 // 4) + 1, jnp.int32)
        _ctx_2048P = jax.random.normal(jax.random.fold_in(_rk, 11), (16, 16, 512), jnp.float32)
        _ctx_2048c = jax.random.dirichlet(jax.random.fold_in(_rk, 511), 0.3 * jnp.ones((16,), jnp.float32), (16, 256))
        _ctx_2048t = jnp.einsum('bsk,bkd->bsd', _ctx_2048c, _ctx_2048P)
        _ctx_2048t = _ctx_2048t * jax.lax.rsqrt(jnp.mean(jnp.square(_ctx_2048t)) + 1e-12) * 0.953939
        ctx_2048 = 4.13588e-05 + 0.999923 * (_ctx_2048t + 0.3 * jax.random.normal(jax.random.fold_in(_rk, 611), (16, 256, 512), jnp.float32))
        _validS = jnp.arange(256)[None, :] < _lenS[:, None]
        _validS2 = jnp.arange(256)[None, :] < _lenS2[:, None]
        _causal = jnp.tril(jnp.ones((256, 256), dtype=bool))
        mask_SxS2_bc0 = jnp.logical_not(jnp.broadcast_to(_validS2[0:1, :], (256, 256)))
        mask_BxS2_bk0 = jnp.logical_not(jnp.broadcast_to(_validS2[:, :], (16, 256)))
        return (x, ctx_2048, mask_SxS2_bc0, mask_BxS2_bk0)
    x, ctx_2048, mask_SxS2_bc0, mask_BxS2_bk0 = _rec_inputs()

    def _L0_attn_setup():
        import jax, jax.numpy as jnp
        import numpy as np
        D_MODEL = 512
        HEADS = 16
        HEAD_DIM = D_MODEL // HEADS
        key = jax.random.key(seed)
        k1, k2, k3 = jax.random.split(key, 3)
        B, S = (1, 512)
        x = jax.random.normal(k1, (B, S, D_MODEL), dtype=jnp.float32)
        Wqkv_w = jax.random.normal(k2, (D_MODEL + 2 * HEAD_DIM, D_MODEL), dtype=jnp.float32) * D_MODEL ** (-0.5)
        Wqkv_b = jnp.zeros((D_MODEL + 2 * HEAD_DIM,), dtype=jnp.float32)
        out_w = jax.random.normal(k3, (D_MODEL, D_MODEL), dtype=jnp.float32) * D_MODEL ** (-0.5)
        out_b = jnp.zeros((D_MODEL,), dtype=jnp.float32)
        return {'x': x, 'Wqkv_w': Wqkv_w, 'Wqkv_b': Wqkv_b, 'out_w': out_w, 'out_b': out_b}
    _L0_attn_all = _L0_attn_setup()
    _L0_attn_in = {k: v for k, v in _L0_attn_all.items() if k in ('Wqkv_w', 'Wqkv_b', 'out_w', 'out_b')}
    del _L0_attn_all

    def _L0_xattn_setup():
        import jax, jax.numpy as jnp
        import numpy as np
        B, LQ, LKV = (4, 256, 256)
        HID, H, G = (512, 32, 8)
        HD = HID // H
        HPG = H // G
        key = jax.random.key(seed)
        ks = jax.random.split(key, 10)
        s = 0.02
        inp = {'X': jax.random.normal(ks[0], (B, LQ, HID), jnp.float32), 'encoder_output': jax.random.normal(ks[1], (B, LKV, HID), jnp.float32), 'causal_mask': jnp.triu(jnp.ones((LQ, LKV), bool), 1), 'padding_mask': jnp.zeros((B, LKV), bool).at[B // 2:, LKV - LKV // 4:].set(True), 'Wq': jax.random.normal(ks[2], (HID, HID), jnp.float32) * s, 'bq': jnp.zeros((HID,), jnp.float32), 'Wk': jax.random.normal(ks[3], (G * HD, HID), jnp.float32) * s, 'bk': jnp.zeros((G * HD,), jnp.float32), 'Wv': jax.random.normal(ks[4], (G * HD, HID), jnp.float32) * s, 'bv': jnp.zeros((G * HD,), jnp.float32), 'Wo': jax.random.normal(ks[5], (HID, HID), jnp.float32) * s, 'bo': jnp.zeros((HID,), jnp.float32)}
        return inp
    _L0_xattn_all = _L0_xattn_setup()
    _L0_xattn_in = {k: v for k, v in _L0_xattn_all.items() if k in ('Wq', 'bq', 'Wk', 'bk', 'Wv', 'bv', 'Wo', 'bo')}
    del _L0_xattn_all

    def _L0_ffn_setup():
        import jax, jax.numpy as jnp
        import numpy as np
        key = jax.random.key(seed)
        k1, k2, k3, k4, k5 = jax.random.split(key, 5)
        B, L, H, N = (2, 512, 512, 2048)
        x = jax.random.normal(k1, (B, L, H), dtype=jnp.float32)
        W0 = jax.random.normal(k2, (N, H), dtype=jnp.float32) * (1.0 / np.sqrt(H))
        bias0 = jax.random.normal(k3, (N,), dtype=jnp.float32) * 0.02
        W1 = jax.random.normal(k4, (H, N), dtype=jnp.float32) * (1.0 / np.sqrt(N))
        bias1 = jax.random.normal(k5, (H,), dtype=jnp.float32) * 0.02
        return {'x': x, 'W0': W0, 'bias0': bias0, 'W1': W1, 'bias1': bias1}
    _L0_ffn_all = _L0_ffn_setup()
    _L0_ffn_in = {k: v for k, v in _L0_ffn_all.items() if k in ('W0', 'bias0', 'W1', 'bias1')}
    del _L0_ffn_all
    return {'x': x, 'ctx_2048': ctx_2048, 'mask_SxS2_bc0': mask_SxS2_bc0, 'mask_BxS2_bk0': mask_BxS2_bk0, 'L0_attn_Wqkv_w': _L0_attn_in['Wqkv_w'], 'L0_attn_Wqkv_b': _L0_attn_in['Wqkv_b'], 'L0_attn_out_w': _L0_attn_in['out_w'], 'L0_attn_out_b': _L0_attn_in['out_b'], 'L0_xattn_Wq': _L0_xattn_in['Wq'], 'L0_xattn_bq': _L0_xattn_in['bq'], 'L0_xattn_Wk': _L0_xattn_in['Wk'], 'L0_xattn_bk': _L0_xattn_in['bk'], 'L0_xattn_Wv': _L0_xattn_in['Wv'], 'L0_xattn_bv': _L0_xattn_in['bv'], 'L0_xattn_Wo': _L0_xattn_in['Wo'], 'L0_xattn_bo': _L0_xattn_in['bo'], 'L0_ffn_W0': _L0_ffn_in['W0'], 'L0_ffn_bias0': _L0_ffn_in['bias0'], 'L0_ffn_W1': _L0_ffn_in['W1'], 'L0_ffn_bias1': _L0_ffn_in['bias1']}

def reference(x, ctx_2048, mask_SxS2_bc0, mask_BxS2_bk0, L0_attn_Wqkv_w, L0_attn_Wqkv_b, L0_attn_out_w, L0_attn_out_b, L0_xattn_Wq, L0_xattn_bq, L0_xattn_Wk, L0_xattn_bk, L0_xattn_Wv, L0_xattn_bv, L0_xattn_Wo, L0_xattn_bo, L0_ffn_W0, L0_ffn_bias0, L0_ffn_W1, L0_ffn_bias1):
    import jax
    import jax.numpy as jnp

    def _L0_attn_ref(x, Wqkv_w, Wqkv_b, out_w, out_b):
        import jax, jax.numpy as jnp
        import numpy as np
        D_MODEL = 512
        HEADS = 16
        HEAD_DIM = D_MODEL // HEADS
        B, S, _ = x.shape
        qkv = jnp.einsum('bsd,ed->bse', x, Wqkv_w) + Wqkv_b
        q = qkv[..., :D_MODEL]
        k = qkv[..., D_MODEL:D_MODEL + HEAD_DIM]
        v = qkv[..., D_MODEL + HEAD_DIM:]
        q = q.reshape(B, S, HEADS, HEAD_DIM)
        scale = 1.0 / np.sqrt(HEAD_DIM)
        scores = jnp.einsum('bqhd,bkd->bhqk', q, k) * scale
        min_val = jnp.finfo(scores.dtype).min
        causal = jnp.tril(jnp.ones((S, S), dtype=bool))
        scores = jnp.where(causal[None, None], scores, min_val)
        attn = jax.nn.softmax(scores, axis=-1)
        ctx = jnp.einsum('bhqk,bkd->bqhd', attn, v)
        ctx = ctx.reshape(B, S, D_MODEL)
        out = jnp.einsum('bsd,ed->bse', ctx, out_w) + out_b
        return out

    def _L0_xattn_ref(X, encoder_output, causal_mask, padding_mask, Wq, bq, Wk, bk, Wv, bv, Wo, bo):
        import jax, jax.numpy as jnp
        import numpy as np
        B, LQ, LKV = (4, 256, 256)
        HID, H, G = (512, 32, 8)
        HD = HID // H
        HPG = H // G
        b = X.shape[0]
        q = X @ Wq.T + bq
        k = encoder_output @ Wk.T + bk
        v = encoder_output @ Wv.T + bv
        q = q.reshape(b, LQ, G, HPG, HD).transpose(0, 2, 3, 1, 4)
        k = k.reshape(b, LKV, G, HD).transpose(0, 2, 1, 3)
        v = v.reshape(b, LKV, G, HD).transpose(0, 2, 1, 3)
        scores = jnp.einsum('bgrqd,bgkd->bgrqk', q, k) / jnp.sqrt(jnp.float32(HD))
        scores = jnp.where(causal_mask[None, None, None, :, :], -jnp.inf, scores)
        scores = jnp.where(padding_mask[:, None, None, None, :], -jnp.inf, scores)
        w = jax.nn.softmax(scores, axis=-1)
        out = jnp.einsum('bgrqk,bgkd->bgrqd', w, v)
        out = out.reshape(b, H, LQ, HD).transpose(0, 2, 1, 3).reshape(b, LQ, HID)
        return out @ Wo.T + bo

    def _L0_ffn_ref(x, W0, bias0, W1, bias1):
        import jax, jax.numpy as jnp
        import numpy as np
        B, L, H = x.shape
        X = x.reshape(-1, H).astype(jnp.float16)
        D = jnp.dot(X.astype(jnp.float32), W0.T) + bias0
        D = jax.nn.gelu(D, approximate=False).astype(jnp.float16)
        E = jnp.dot(D.astype(jnp.float32), W1.T) + bias1
        return E.astype(jnp.float16).reshape(B, L, H)
    x = x + _L0_attn_ref(_layernorm(x, axis=-1), L0_attn_Wqkv_w, L0_attn_Wqkv_b, L0_attn_out_w, L0_attn_out_b)
    x = x + _L0_xattn_ref(_layernorm(x, axis=-1), ctx_2048, mask_SxS2_bc0, mask_BxS2_bk0, L0_xattn_Wq, L0_xattn_bq, L0_xattn_Wk, L0_xattn_bk, L0_xattn_Wv, L0_xattn_bv, L0_xattn_Wo, L0_xattn_bo)
    x = x + _L0_ffn_ref(_layernorm(x, axis=-1), L0_ffn_W0, L0_ffn_bias0, L0_ffn_W1, L0_ffn_bias1)
    return x

_drawn_inputs = setup_inputs


def setup_inputs(seed=0):
    import zlib

    import numpy as np

    out = dict(_drawn_inputs(seed))
    spreads = {'L0_attn_Wqkv_b': (0.0, 0.1),
     'L0_attn_out_b': (0.0, 0.1),
     'L0_xattn_bq': (0.0, 0.8),
     'L0_xattn_bk': (0.0, 0.8),
     'L0_xattn_bv': (0.0, 0.1),
     'L0_xattn_bo': (0.0, 0.1)}
    factors = {'L0_xattn_Wq': 8.0, 'L0_xattn_Wk': 8.0, 'L0_ffn_bias0': 5.18, 'L0_ffn_bias1': 3.708}
    for name, (base, spread) in spreads.items():
        noise = np.random.default_rng([zlib.crc32(name.encode()), seed]).standard_normal(out[name].shape)
        drawn = base * np.exp(spread * noise) if base else spread * noise
        out[name] = jnp.asarray(drawn.astype(out[name].dtype))
    for name, factor in factors.items():
        out[name] = (out[name] * factor).astype(out[name].dtype)
    return out
```

```python
from contextlib import ExitStack

import concourse.bass as bass
from concourse import mybir

ALU = mybir.AluOpType
ACT = mybir.ActivationFunctionType
AX = mybir.AxisListType
F32 = mybir.dt.float32
F32R = mybir.dt.float32r
BF16 = mybir.dt.bfloat16
F16 = mybir.dt.float16
U32 = mybir.dt.uint32
U8 = mybir.dt.uint8

P = 128
D = 512
DC = D // P
S = 256
NT = S // P
BIG = 1e30
SHIFT_MAX = 1e29
EPS = 1e-5
STACK = 97


class Attention:

    def __init__(self, name, head_dim, causal):
        self.name = name
        self.HD = head_dim
        self.NB = P // head_dim
        self.NH = self.NB * DC
        self.causal = causal
        self.VD = head_dim if causal else P
        self.KD = P
        self.scale = float(head_dim) ** -0.5
        self.shift_row = 3 * head_dim
        self.max_units = []
        for qt in range(NT):
            width = P * (qt + 1) if causal else S
            n = 512 // width
            self.max_units += [(qt, c, b, n, width) for c in range(DC) for b in range(0, self.NB, n)]
        self.quads = []
        for qt in range(NT):
            for half in range(self.NB // 4):
                blocks = [4 * 0 + b for b in range(4)] if causal else [2 * j + half for j in range(4)]
                key_tiles = range(qt + 1) if causal else range(NT)
                self.quads.append((qt, half, blocks, list(key_tiles)))
        self.score_units = [(n, kt, j) for n, (_, _, _, kts) in enumerate(self.quads) for kt in kts for j in range(4)]
        assert len(self.score_units) == len(self.max_units)
        self.n_units = len(self.max_units)
        self.quad_end = []
        end = 0
        for _, _, _, kts in self.quads:
            end += 4 * len(kts)
            self.quad_end.append(end)
        self.pv_after = {}
        for n in range(len(self.quads) - 1):
            self.pv_after[self.quad_end[n] + 2] = n
        self.n_shuffles = 3 * self.NB + 3 * (1 if causal else self.NB)


def wait(engine, sem, value):
    if isinstance(value, int) and value <= 0:
        return
    engine.wait_ge(sem, value)


def spread(ap, times):
    return ap.unsqueeze(1).broadcast_to([ap.shape[0], times, ap.shape[1]])


def build_attention(nc, A, B, x_in, x_out, w, ctx_t=None, mask=None, mask_t=None, pad=None, pad_col=None):
    HD, NB, VD, NH = A.HD, A.NB, A.VD, A.NH
    cross = not A.causal
    NU, NQ = A.n_units, len(A.quads)
    with ExitStack() as es:
        def sb(name, shape, dt):
            return es.enter_context(nc.sbuf_tensor(f"{A.name}_{name}", shape, dt))

        def pb(name, shape, dt=F32):
            return es.enter_context(nc.psum_tensor(f"{A.name}_{name}", shape, dt))

        def sem(name):
            return es.enter_context(nc.semaphore(f"{A.name}_{name}"))

        stage = sb("stage", [P, DC, D], F32)
        wq = [sb(f"wq{n}", [P, DC, D], F32R) for n in range(2)]
        wkv = [sb(f"wkv{n}", [P, DC, P + VD], F32R) for n in range(2)]
        wo = [sb(f"wo{n}", [P, DC, D], F32R) for n in range(2)]
        bq = sb("bq", [P, DC], F32)
        bk = sb("bk", [P, 1], F32)
        bv = sb("bv", [P, VD], F32)
        bo = sb("bo", [P, D], F32)
        ident = sb("ident", [P, P], F32)
        ident16 = sb("ident16", [P, P], BF16)
        block_mask = sb("block_mask", [P, NB], F32)
        ones_v = sb("ones_v", [P, 2, 32], F32)
        ones_row = sb("ones_row", [1, NB * S], F32R)
        mask_q0 = sb("mask_q0", [P, NT, S], BF16)
        mask_k0 = sb("mask_k0", [P, NT, S], BF16)
        x_tile = sb("x_tile", [P, NT, D], F32)
        stats = sb("stats", [P, NT, 6], F32)
        mv = sb("mv", [P, NT, 2], F32)
        veps = sb("veps", [P, NT], F32)
        lnv = sb("lnv", [P, NT], F32)
        r0 = sb("r0", [P, NT], F32)
        r1 = sb("r1", [P, NT], F32)
        r2 = sb("r2", [P, NT], F32)
        gate = sb("gate", [P, 1], F32)
        rstd = sb("rstd", [P, NT], F32)
        xn = sb("xn", [P, NT, D], F32)
        xt = [sb(f"xt{n}", [P, DC, S], F32R) for n in range(2)]
        qt_ = [sb(f"qt{n}", [P, DC, S], F32R) for n in range(2)]
        kt_ = [sb(f"kt{n}", [P, S], F32R) for n in range(2)]
        k_blocks = sb("k_blocks", [P, NB, S], F32R)
        v_new = sb("v_new", [P, NT, VD], F32)
        v_use = sb("v_use", [P, NT, 1 if A.causal else NB, 32], F32)
        row_max = sb("row_max", [P, NT, NB, DC], F32)
        shift = sb("shift", [P, NT, NH], F32)
        shift_t = sb("shift_t", [NH, S], F32R)
        q_stack = sb("q_stack", [STACK, NB * DC, S], F32R)
        k_stack = sb("k_stack", [STACK, 1 if A.causal else NB, S], F32R)
        probs = sb("probs", [P, 2, NT, 4, 512], F32)
        recip = sb("recip", [P, 512], F32)
        heads = sb("heads", [P, NT, 512], F32)
        ht = [sb(f"ht{n}", [P, NT, DC, P], F32R) for n in range(2)]
        x_res = sb("x_res", [P, NT, D], F32)
        x_new = sb("x_new", [P, NT, D], F32)
        if cross:
            src = stage[:, :, 0:S]
            ct = [sb(f"ct{n}", [P, DC, S], F32R) for n in range(2)]
            mask_words = sb("mask_words", [P, 2, NT, S // 4], U32)
            pad_words = sb("pad_words", [P, S // 4], U32)
            pad_f = sb("pad_f", [P, S], F32)
            padc_words = sb("padc_words", [P, B * NT // 4], U32)
            padc_f = sb("padc_f", [P, B * NT], F32)
            mask_q = sb("mask_q", [P, NT, S], BF16)
            mask_k = sb("mask_k", [P, NT, S], BF16)
            kv_src = ct
        else:
            mask_q, mask_k, kv_src = mask_q0, mask_k0, xt

        proj = [pb(f"proj{n}", [P, 512]) for n in range(2)]
        max_ps = [pb(f"max{n}", [P, 512]) for n in range(2)]
        score_ps = [pb(f"score{n}", [P, 512]) for n in range(2)]
        heads_ps = pb("heads_ps", [P, 512])
        sums_ps = pb("sums_ps", [P, 512])

        shift_rows = nc.dram_tensor(f"{A.name}_shift_rows", [1, NH, S], F32, kind="Internal").ap()
        shift_spilled = sem("shift_spilled")
        biases_in, masks_in, ones_in = sem("biases_in"), sem("masks_in"), sem("ones_in")
        w_in, w_hi, w_lo = sem("w_in"), sem("w_hi"), sem("w_lo")
        ident_set, masks_set, consts_set, stacks_set = sem("ident_set"), sem("masks_set"), sem("consts_set"), sem("stacks_set")
        x_loaded, src_loaded, pad_loaded = sem("x_loaded"), sem("src_loaded"), sem("pad_loaded")
        ln_step, var_ready, ln_done, rsqrt_done, xn_ready = sem("ln_step"), sem("var_ready"), sem("ln_done"), sem("rsqrt_done"), sem("xn_ready")
        t_ready, xt_hi, xt_lo = sem("t_ready"), sem("xt_hi"), sem("xt_lo")
        ct_hi, ct_lo = sem("ct_hi"), sem("ct_lo")
        q_ready, q_hi, q_lo = sem("q_ready"), sem("q_hi"), sem("q_lo")
        k_ready, k_hi, k_lo, kb_ready = sem("k_ready"), sem("k_hi"), sem("k_lo"), sem("kb_ready")
        v_ready, v_done = sem("v_ready"), sem("v_done")
        padf_set, mask_q_ready, mask_k_ready = sem("padf_set"), sem("mask_q_ready"), sem("mask_k_ready")
        max_ready, max_done, shift_ready, shift_t_ready, shift_t_done = (
            sem("max_ready"), sem("max_done"), sem("shift_ready"), sem("shift_t_ready"), sem("shift_t_done"))
        stacked, shift_stacked, v_use_ready = sem("stacked"), sem("shift_stacked"), sem("v_use_ready")
        score_ready, exp_done, pv_done = sem("score_ready"), sem("exp_done"), sem("pv_done")
        recip_done, heads_ready, ht_hi, ht_lo = sem("recip_done"), sem("heads_ready"), sem("ht_hi"), sem("ht_lo")
        res_loaded, res_biased, o_ready, o_done, stored = (
            sem("res_loaded"), sem("res_biased"), sem("o_ready"), sem("o_done"), sem("stored"))
        block = es.enter_context(nc.Block())

        def tiles(dram, i):
            return dram[bass.ds(i, 1), :, :].rearrange("a (t p) d -> p (a t) d", p=P)

        def steps(engine, step):
            step(-1, False, False, True)
            step(0, True, False, True)
            step(1, True, True, True)
            with engine.Fori(2, B - 1) as i:
                step(i, True, True, True)
            step(B - 1, True, True, False)
            step(B, False, True, False)

        @block.sync
        def _(sp):
            pieces = [(stage[:, :, :], w["q"].rearrange("(c p) n -> p c n", p=P))]
            kv = w["kv"]
            sp.dma_start(pieces[0][0], pieces[0][1]).then_inc(w_in, 16)
            sp.dma_start(bq[:, :], w["bq"]).then_inc(biases_in, 16)
            sp.dma_start(bk[:, :], w["bk"]).then_inc(biases_in, 16)
            sp.dma_start(bv[:, :], w["bv"].partition_broadcast(P)).then_inc(biases_in, 16)
            sp.dma_start(bo[:, :], w["bo"].partition_broadcast(P)).then_inc(biases_in, 16)
            if cross:
                sp.dma_start(mask_words[:, 0], mask.rearrange("(t p) k -> p t k", p=P)).then_inc(masks_in, 16)
                sp.dma_start(mask_words[:, 1], mask_t.rearrange("(t p) q -> p t q", p=P)).then_inc(masks_in, 16)
                sp.dma_start(padc_words[:, :], pad_col).then_inc(masks_in, 16)
            sp.wait_ge(w_lo, 1)
            sp.dma_start(stage[:, :, 0:P + VD], kv.rearrange("(c p) n -> p c n", p=P)).then_inc(w_in, 16)
            sp.wait_ge(w_lo, 2)
            sp.dma_start(stage[:, :, :], w["o"].rearrange("(c p) n -> p c n", p=P)).then_inc(w_in, 16)
            sp.wait_ge(stacks_set, 3)
            sp.dma_start(k_stack[A.shift_row:A.shift_row + 1, :, :].bitcast(F32),
                         ones_row[0:1, 0:k_stack.shape[1] * S].rearrange("a (n s) -> a n s", s=S).bitcast(F32)).then_inc(ones_in, 16)

            def step(i, mx, st, tq):
                b, n = i - 1, i + 1
                if st:
                    wait(sp, o_done, 2 * b)
                    sp.dma_start(x_res[:, :, :], tiles(x_in, b)).then_inc(res_loaded, 16)
                if tq:
                    wait(sp, xn_ready, 2 * n)
                    sp.dma_start(x_tile[:, :, :], tiles(x_in, n)).then_inc(x_loaded, 16)
                    if cross:
                        wait(sp, ct_lo, n)
                        sp.dma_start(src, ctx_t[bass.ds(n, 1), :, :].rearrange("a (c p) s -> p (a c) s", p=P)).then_inc(src_loaded, 16)
                        wait(sp, padf_set, n)
                        sp.dma_start(pad_words[:, :], pad[bass.ds(n, 1), :].rearrange("a s -> (a s)").partition_broadcast(P)).then_inc(pad_loaded, 16)
                if mx:
                    if st:
                        wait(sp, score_ready, NU * (b + 1))
                    wait(sp, k_lo, i + 1)
                    for part, rows in ((0, 0), (1, 1), (0, 2)):
                        for g in range(NB):
                            sp.dma_start(q_stack[rows * HD:(rows + 1) * HD, g * DC:(g + 1) * DC, :].bitcast(F32),
                                         qt_[part][g * HD:(g + 1) * HD, :, :].bitcast(F32)).then_inc(stacked, 16)
                    for part, rows in ((0, 0), (0, 1), (1, 2)):
                        for g in range(k_stack.shape[1]):
                            sp.dma_start(k_stack[rows * HD:(rows + 1) * HD, g, :].bitcast(F32),
                                         kt_[part][g * HD:(g + 1) * HD, :].bitcast(F32)).then_inc(stacked, 16)
                    wait(sp, shift_t_done, i + 1)
                    sp.dma_start(shift_rows[0, :, :], shift_t[:, :].bitcast(F32)).then_inc(shift_spilled, 16)
                    wait(sp, shift_spilled, 16 * (i + 1))
                    sp.dma_start(q_stack[A.shift_row:A.shift_row + 1, 0:NH, :].bitcast(F32), shift_rows).then_inc(shift_stacked, 16)
                if st:
                    wait(sp, o_done, 2 * (b + 1))
                    sp.dma_start(tiles(x_out, b), x_new[:, :, :]).then_inc(stored, 16)

            sp.wait_ge(w_lo, 3)
            steps(sp, step)
            sp.wait_ge(stored, 16 * B)

        @block.gpsimd
        def _(pool):
            pool.memset(ident[:, :], 0.0).then_inc(ident_set, 1)
            pool.memset(mask_q0[:, :, :], 0.0).then_inc(ident_set, 1)
            pool.memset(mask_k0[:, :, :], 0.0).then_inc(ident_set, 1)
            pool.memset(block_mask[:, :], 1.0).then_inc(ident_set, 1)
            pool.wait_ge(ident_set, 4)
            pool.affine_select(out=ident[:, :], in_=ident[:, :], compare_op=ALU.not_equal, fill=1.0, base=0,
                               pattern=[[-1, P]], channel_multiplier=1).then_inc(ident_set, 1)
            pool.affine_select(out=block_mask[:, :], in_=block_mask[:, :], compare_op=ALU.is_ge, fill=0.0, base=0,
                               pattern=[[-HD, NB]], channel_multiplier=1).then_inc(ident_set, 1)
            pool.wait_ge(ident_set, 6)
            pool.affine_select(out=block_mask[:, :], in_=block_mask[:, :], compare_op=ALU.is_ge, fill=0.0, base=HD - 1,
                               pattern=[[HD, NB]], channel_multiplier=-1).then_inc(ident_set, 1)
            if A.causal:
                pool.affine_select(out=mask_q0[:, :, :], in_=mask_q0[:, :, :], compare_op=ALU.is_ge, fill=-BIG, base=0,
                                   pattern=[[P, NT], [-1, S]], channel_multiplier=1).then_inc(masks_set, 1)
                pool.affine_select(out=mask_k0[:, :, :], in_=mask_k0[:, :, :], compare_op=ALU.is_ge, fill=-BIG, base=0,
                                   pattern=[[-P, NT], [1, S]], channel_multiplier=-1).then_inc(masks_set, 1)

            def step(i, mx, st, tq):
                b = i - 1
                if st:
                    wait(pool, res_loaded, 16 * (b + 1))
                    if isinstance(i, int) and i == 1:
                        pool.wait_ge(biases_in, 64)
                    pool.tensor_tensor(x_res[:, :, :], x_res[:, :, :], spread(bo[:, :], NT), ALU.add).then_inc(res_biased, 1)

            steps(pool, step)

        @block.scalar
        def _(act):
            for n, (part, width) in enumerate(((wq, D), (wkv, P + VD), (wo, D))):
                act.wait_ge(w_in, 16 * (n + 1))
                act.activation(part[0][:, :, :], stage[:, :, 0:width], ACT.Copy).then_inc(w_hi, 1)
            act.wait_ge(biases_in, 64)

            def rsqrt_guess(n):
                wait(act, var_ready, n + 1)
                act.activation(lnv[:, :], veps[:, :], ACT.Ln).then_inc(ln_done, 1)
                wait(act, ln_done, n + 1)
                act.activation(r0[:, :], lnv[:, :], ACT.Exp, scale=-0.5).then_inc(rsqrt_done, 1)

            def step(i, mx, st, tq):
                b, n = i - 1, i + 1
                if st:
                    for u, (quad, kt, j) in enumerate(A.score_units):
                        if u == 4 and tq:
                            rsqrt_guess(n)
                        if kt == 0 and j == 0:
                            wait(act, pv_done, NQ * b + quad - 1)
                        wait(act, score_ready, NU * b + u + 1)
                        act.activation(probs[:, quad % 2, kt, j, :], score_ps[u % 2][:, :], ACT.Exp, scale=A.scale).then_inc(exp_done, 1)
                elif tq:
                    rsqrt_guess(n)
                if mx:
                    wait(act, shift_t_ready, i + 1)
                    wait(act, shift_stacked, 16 * i)
                    act.activation(shift_t[:, :], proj[0][0:NH, 0:S], ACT.Copy).then_inc(shift_t_done, 1)
                if st:
                    for t in range(NT):
                        wait(act, heads_ready, NT * b + t + 1)
                        wait(act, o_ready, NT * b)
                        act.activation(ht[0][:, t, :, :], heads[:, t, :].rearrange("p (c q) -> p c q", c=DC), ACT.Copy).then_inc(ht_hi, 1)
                if tq:
                    if cross:
                        wait(act, src_loaded, 16 * (n + 1))
                        wait(act, v_ready, n)
                        act.activation(ct[0][:, :, :], src, ACT.Copy).then_inc(ct_hi, 1)
                    for t in range(NT):
                        wait(act, t_ready, NT * n + t + 1)
                        act.activation(xt[0][:, :, t * P:(t + 1) * P], proj[t][:, :].rearrange("p (c q) -> p c q", c=DC), ACT.Copy).then_inc(xt_hi, 1)
                    for c in range(DC):
                        wait(act, q_ready, DC // 2 * n + c // 2 + 1)
                        if c == 0:
                            wait(act, stacked, 16 * A.n_shuffles * n)
                            wait(act, max_ready, NU * n)
                        act.activation(qt_[0][:, c, :], proj[c // 2][:, (c % 2) * S:(c % 2 + 1) * S], ACT.Identity, bias=bq[:, c:c + 1]).then_inc(q_hi, 1)
                    wait(act, k_ready, n + 1)
                    act.activation(kt_[0][:, :], proj[0][:, 0:S], ACT.Identity, bias=bk[:, 0:1]).then_inc(k_hi, 1)

            steps(act, step)

        @block.vector
        def _(dve):
            for n, (part, width) in enumerate(((wq, D), (wkv, P + VD), (wo, D))):
                dve.wait_ge(w_hi, n + 1)
                dve.tensor_tensor(part[1][:, :, :], stage[:, :, 0:width], part[0][:, :, :].bitcast(F32), ALU.subtract).then_inc(w_lo, 1)
            dve.memset(q_stack[:, :, :].bitcast(F32), 0.0).then_inc(stacks_set, 1)
            dve.memset(k_stack[:, :, :].bitcast(F32), 0.0).then_inc(stacks_set, 1)
            dve.memset(ones_row[:, :].bitcast(F32), 1.0).then_inc(stacks_set, 1)
            dve.memset(v_use[:, :, :, :], 0.0).then_inc(consts_set, 1)
            if cross:
                dve.memset(ones_v[:, :, :], 0.0).then_inc(consts_set, 1)
                dve.wait_ge(consts_set, 2)
                dve.memset(ones_v[:, 0, 0:HD], 1.0).then_inc(consts_set, 1)
                dve.memset(ones_v[:, 1, HD:2 * HD], 1.0).then_inc(consts_set, 1)
                dve.wait_ge(masks_in, 48)
                dve.wait_ge(ident_set, 7)
                dve.tensor_scalar(mask_q0[:, :, :], mask_words[:, 0].bitcast(U8), -BIG, None, ALU.mult).then_inc(consts_set, 1)
                dve.tensor_scalar(mask_k0[:, :, :], mask_words[:, 1].bitcast(U8), -BIG, None, ALU.mult).then_inc(consts_set, 1)
                dve.tensor_scalar(padc_f[:, :], padc_words[:, :].bitcast(U8), -BIG, None, ALU.mult).then_inc(consts_set, 1)
            else:
                dve.memset(ones_v[:, :, :], 1.0).then_inc(consts_set, 1)
            dve.wait_ge(ident_set, 7)
            dve.tensor_copy(ident16[:, :], ident[:, :]).then_inc(consts_set, 1)
            dve.wait_ge(consts_set, 8 if cross else 3)
            dve.wait_ge(biases_in, 64)

            def norm_stats(n):
                wait(dve, x_loaded, 16 * (n + 1))
                for t in range(NT):
                    dve.bn_stats(stats[:, t, :], x_tile[:, t, :]).then_inc(ln_step, 1)
                wait(dve, ln_step, 8 * n + 2)
                dve.memset(gate[:, :], 0.0)
                for t in range(NT):
                    dve.bn_aggr(mv[:, t, :], stats[:, t, :]).then_inc(ln_step, 1)
                wait(dve, ln_step, 8 * n + 4)
                dve.tensor_scalar(veps[:, :], mv[:, :, 1], EPS, None, ALU.add).then_inc(var_ready, 1)

            def norm_apply(n):
                wait(dve, rsqrt_done, n + 1)
                dve.tensor_tensor(r1[:, :], r0[:, :], r0[:, :], ALU.mult).then_inc(ln_step, 1)
                wait(dve, ln_step, 8 * n + 5)
                dve.tensor_tensor(r2[:, :], r1[:, :], veps[:, :], ALU.mult).then_inc(ln_step, 1)
                wait(dve, ln_step, 8 * n + 6)
                dve.tensor_scalar(r1[:, :], r2[:, :], -0.5, 1.5, ALU.mult, ALU.add).then_inc(ln_step, 1)
                wait(dve, ln_step, 8 * n + 7)
                dve.tensor_tensor(rstd[:, :], r1[:, :], r0[:, :], ALU.mult).then_inc(ln_step, 1)
                wait(dve, ln_step, 8 * n + 8)
                wait(dve, t_ready, NT * n)
                for t in range(NT):
                    dve.tensor_scalar(xn[:, t, :], x_tile[:, t, :], mv[:, t, 0:1], rstd[:, t:t + 1], ALU.subtract, ALU.mult).then_inc(xn_ready, 1)

            def normalise(b, t):
                quads = NB // 4 * (t + 1)
                wait(dve, pv_done, NQ * b + quads)
                dve.reciprocal(recip[:, :], sums_ps[:, :]).then_inc(recip_done, 1)
                wait(dve, recip_done, NT * b + t + 1)
                wait(dve, ht_hi, NT * b)
                dve.tensor_tensor(heads[:, t, :], heads_ps[:, :], recip[:, :], ALU.mult).then_inc(heads_ready, 1)

            def step(i, mx, st, tq):
                b, n = i - 1, i + 1
                if not mx and tq:
                    norm_stats(n)
                    norm_apply(n)
                for u, (qt, c, blk, nb, width) in enumerate(A.max_units):
                    if mx and tq and u == 2:
                        norm_stats(n)
                    if mx and tq and u == 8:
                        norm_apply(n)
                    if mx:
                        wait(dve, max_ready, NU * i + u + 1)
                        dve.tensor_reduce(row_max[:, qt, blk:blk + nb, c], max_ps[u % 2][:, :].rearrange("p (b k) -> p b k", b=nb),
                                          AX.X, ALU.max).then_inc(max_done, 1)
                    if st and u in A.pv_after and (A.pv_after[u] + 1) % (NB // 4) == 0:
                        normalise(b, (A.pv_after[u] + 1) // (NB // 4) - 1)
                if mx:
                    wait(dve, max_done, NU * (i + 1))
                    wait(dve, shift_t_ready, i)
                    dve.tensor_scalar(shift[:, :, :].rearrange("p t (g c) -> p t g c", c=DC), row_max[:, :, :, :], -1.0, SHIFT_MAX,
                                      ALU.mult, ALU.min).then_inc(shift_ready, 1)
                if st:
                    normalise(b, NT - 1)
                    for t in range(NT):
                        wait(dve, ht_hi, NT * b + t + 1)
                        wait(dve, o_ready, NT * b)
                        dve.tensor_tensor(ht[1][:, t, :, :].rearrange("p c q -> p (c q)"), heads[:, t, :],
                                          ht[0][:, t, :, :].rearrange("p c q -> p (c q)").bitcast(F32), ALU.subtract).then_inc(ht_lo, 1)
                if mx:
                    if st:
                        wait(dve, pv_done, NQ * (b + 1))
                    wait(dve, v_done, i + 1)
                    if A.causal:
                        dve.tensor_copy(v_use[:, :, 0, :], v_new[:, :, :]).then_inc(v_use_ready, 1)
                    else:
                        for half in range(2):
                            dve.tensor_copy(v_use[:, :, half:NB:2, half * HD:(half + 1) * HD],
                                            v_new[:, :, :].rearrange("p t (j h d) -> p t j h d", h=2, d=HD)[:, :, :, half, :]).then_inc(v_use_ready, 1)
                        if st:
                            wait(dve, score_ready, NU * (b + 1))
                        for kt in range(NT):
                            dve.tensor_scalar(mask_k[:, kt, :], mask_k0[:, kt, :], padc_f[:, bass.ds(i * NT + kt, 1)], None, ALU.add).then_inc(mask_k_ready, 1)
                if st:
                    wait(dve, stored, 16 * b)
                    wait(dve, res_biased, b + 1)
                    for t in range(NT):
                        wait(dve, o_ready, NT * b + t + 1)
                        dve.tensor_tensor(x_new[:, t, :], proj[t][:, :], x_res[:, t, :], ALU.add).then_inc(o_done, 1)
                if tq:
                    if cross:
                        wait(dve, ct_hi, n + 1)
                        dve.tensor_tensor(ct[1][:, :, :], src, ct[0][:, :, :].bitcast(F32), ALU.subtract).then_inc(ct_lo, 1)
                    for t in range(NT):
                        wait(dve, xt_hi, NT * n + t + 1)
                        dve.tensor_tensor(xt[1][:, :, t * P:(t + 1) * P], proj[t][:, :].rearrange("p (c q) -> p c q", c=DC),
                                          xt[0][:, :, t * P:(t + 1) * P].bitcast(F32), ALU.subtract).then_inc(xt_lo, 1)
                    for c in range(DC):
                        wait(dve, q_hi, DC * n + c - c % 2 + 2)
                        dve.scalar_tensor_tensor(out=qt_[1][:, c, :], in0=proj[c // 2][:, (c % 2) * S:(c % 2 + 1) * S], scalar=bq[:, c:c + 1],
                                                 in1=qt_[0][:, c, :].bitcast(F32), op0=ALU.add, op1=ALU.subtract).then_inc(q_lo, 1)
                    wait(dve, k_hi, n + 1)
                    dve.scalar_tensor_tensor(out=kt_[1][:, :], in0=proj[0][:, 0:S], scalar=bk[:, 0:1],
                                             in1=kt_[0][:, :].bitcast(F32), op0=ALU.add, op1=ALU.subtract).then_inc(k_lo, 1)
                    wait(dve, max_ready, NU * n)
                    dve.tensor_tensor(k_blocks[:, :, :], spread(kt_[0][:, :].bitcast(F32), NB),
                                      block_mask[:, :].unsqueeze(2).broadcast_to([P, NB, S]), ALU.mult).then_inc(kb_ready, 1)
                    wait(dve, v_ready, n + 1)
                    dve.tensor_tensor(v_new[:, :, :], proj[1][:, 0:NT * VD].rearrange("p (t v) -> p t v", t=NT), spread(bv[:, :], NT), ALU.add).then_inc(v_done, 1)
                    if cross:
                        wait(dve, pad_loaded, 16 * (n + 1))
                        dve.tensor_scalar(pad_f[:, :], pad_words[:, :].bitcast(U8), -BIG, None, ALU.mult).then_inc(padf_set, 1)
                        wait(dve, padf_set, n + 1)
                        dve.tensor_tensor(mask_q[:, :, :], mask_q0[:, :, :], spread(pad_f[:, :], NT), ALU.add).then_inc(mask_q_ready, 1)

            steps(dve, step)

        @block.tensor
        def _(pe):
            pe.wait_ge(consts_set, 8 if cross else 3)
            if A.causal:
                pe.wait_ge(masks_set, 2)
            pe.wait_ge(w_lo, 3)
            pe.wait_ge(ones_in, 16)

            def three(out, a, b, first, last):
                for k, (x, y) in enumerate(((0, 0), (1, 0), (0, 1))):
                    mm = pe.matmul(out, a[x], b[y], start=first and k == 0, stop=last and k == 2)
                return mm

            def max_unit(i, u):
                qt, c, blk, nb, width = A.max_units[u]
                if u == 0:
                    wait(pe, kb_ready, i + 1)
                    wait(pe, q_hi, DC * (i + 1))
                    if cross:
                        wait(pe, mask_q_ready, i + 1)
                wait(pe, max_done, NU * i + u - 1)
                out = max_ps[u % 2][:, :]
                pe.matmul(out, qt_[0][:, c, qt * P:(qt + 1) * P], k_blocks[:, blk:blk + nb, 0:width], start=True, stop=False)
                pe.matmul(out, ident16[:, :], spread(mask_q[:, qt, 0:width], nb), start=False, stop=True).then_inc(max_ready, 1)

            def score_unit(b, u):
                quad, kt, j = A.score_units[u]
                qt, half, blocks, _ = A.quads[quad]
                g = blocks[j]
                masked = cross or kt == qt
                if u == 0:
                    wait(pe, stacked, 16 * A.n_shuffles * (b + 1))
                    wait(pe, shift_stacked, 16 * (b + 1))
                    if cross:
                        wait(pe, mask_k_ready, NT * (b + 1))
                wait(pe, exp_done, NU * b + u - 1)
                out = score_ps[u % 2][:, :]
                mm = pe.matmul(out, k_stack[:, 0 if A.causal else g, kt * P:(kt + 1) * P],
                               q_stack[:, g * DC:(g + 1) * DC, qt * P:(qt + 1) * P], start=True, stop=not masked)
                if masked:
                    mm = pe.matmul(out, ident16[:, :], spread(mask_k[:, kt, qt * P:(qt + 1) * P], DC), start=False, stop=True)
                mm.then_inc(score_ready, 1)

            def pv_quad(b, quad):
                qt, half, blocks, kts = A.quads[quad]
                wait(pe, exp_done, NU * b + A.quad_end[quad])
                if quad == 0:
                    wait(pe, v_use_ready, (1 if A.causal else 2) * (b + 1))
                if half == 0:
                    wait(pe, heads_ready, NT * b + qt)
                last_half = NB // 4 - 1
                for kt in kts:
                    for out_ps, w_of in ((heads_ps, lambda g: v_use[:, kt, 0 if A.causal else g, :]), (sums_ps, lambda g: ones_v[:, half, :])):
                        for j, g in enumerate(blocks):
                            mm = pe.matmul(out_ps[32 * j:32 * j + 32, :], w_of(g), probs[:, quad % 2, kt, j, :],
                                           start=(half == 0 and kt == 0), stop=(half == last_half and kt == kts[-1]),
                                           tile_position=(0, 32 * j))
                mm.then_inc(pv_done, 1)

            def step(i, mx, st, tq):
                b, n = i - 1, i + 1
                for u in range(NU):
                    if st:
                        score_unit(b, u)
                    if mx:
                        max_unit(i, u)
                    if st and u in A.pv_after:
                        pv_quad(b, A.pv_after[u])
                if st:
                    pv_quad(b, NQ - 1)
                if mx:
                    wait(pe, shift_ready, i + 1)
                    wait(pe, k_lo, i + 1)
                    for t in range(NT):
                        mm = pe.transpose(proj[0][0:NH, t * P:(t + 1) * P], shift[:, t, :], ident[:, :])
                    mm.then_inc(shift_t_ready, 1)
                if st:
                    for t in range(NT):
                        wait(pe, ht_lo, NT * b + t + 1)
                        if mx:
                            wait(pe, shift_t_done if t == 0 else v_done, i + 1)
                        for c in range(DC):
                            mm = three(proj[t][:, :], [h[:, t, c, :] for h in ht], [h[:, c, :] for h in wo], c == 0, c == DC - 1)
                        mm.then_inc(o_ready, 1)
                if tq:
                    for t in range(NT):
                        wait(pe, xn_ready, NT * n + t + 1)
                        if st:
                            wait(pe, o_done, NT * b + t + 1)
                        elif mx:
                            wait(pe, shift_t_done if t == 0 else v_done, i + 1)
                        for c in range(DC):
                            mm = pe.transpose(proj[t][:, c * P:(c + 1) * P], xn[:, t, c * P:(c + 1) * P], ident[:, :])
                        mm.then_inc(t_ready, 1)
                    wait(pe, xt_lo, NT * (n + 1))
                    for c in range(DC):
                        for k in range(DC):
                            mm = three(proj[c // 2][:, (c % 2) * S:(c % 2 + 1) * S], [h[:, k, c * P:(c + 1) * P] for h in wq],
                                       [h[:, k, :] for h in xt], k == 0, k == DC - 1)
                        if c % 2:
                            mm.then_inc(q_ready, 1)
                    if cross:
                        wait(pe, ct_lo, n + 1)
                    wait(pe, q_lo, DC * n + 2)
                    for k in range(DC):
                        mm = three(proj[0][:, 0:S], [h[:, k, 0:P] for h in wkv], [h[:, k, :] for h in kv_src], k == 0, k == DC - 1)
                    mm.then_inc(k_ready, 1)
                    wait(pe, q_lo, DC * n + 4)
                    for t in range(NT):
                        for k in range(DC):
                            mm = three(proj[1][:, t * VD:(t + 1) * VD], [h[:, k, t * P:(t + 1) * P] for h in kv_src],
                                       [h[:, k, P:P + VD] for h in wkv], k == 0, k == DC - 1)
                    mm.then_inc(v_ready, 1)

            steps(pe, step)


def build_ffn(nc, B, x_in, x_out, w0, b0, w1, b1):
    F = w0.shape[1]
    FC = F // P
    TOK = 512
    TT = TOK // P
    N = B * S // TOK
    RING = 4
    LAG = 2
    with ExitStack() as es:
        def sb(name, shape, dt):
            return es.enter_context(nc.sbuf_tensor(f"ffn_{name}", shape, dt))

        def pb(name, shape, dt=F32):
            return es.enter_context(nc.psum_tensor(f"ffn_{name}", shape, dt))

        def sem(name):
            return es.enter_context(nc.semaphore(f"ffn_{name}"))

        stage = sb("stage", [P, 2, F], F32)
        w0s = [sb(f"w0{n}", [P, DC, F], F32R) for n in range(2)]
        w1s = [sb(f"w1{n}", [P, FC, D], F32R) for n in range(2)]
        bias0 = sb("bias0", [P, FC], F32)
        bias1 = sb("bias1", [P, D], F32)
        ident = sb("ident", [P, P], F32)
        ident16 = sb("ident16", [P, P], F16)
        x_tile = sb("x_tile", [P, TT, D], F32)
        stats = sb("stats", [P, TT, 6], F32)
        mv = sb("mv", [P, TT, 2], F32)
        veps = sb("veps", [P, TT], F32)
        root = sb("root", [P, TT], F32)
        r0 = sb("r0", [P, TT], F32)
        r1 = sb("r1", [P, TT], F32)
        r2 = sb("r2", [P, TT], F32)
        gate = sb("gate", [P, 1], F32)
        rstd = sb("rstd", [P, TT], F32)
        xn = sb("xn", [P, TT, D], F16)
        xt = sb("xt", [P, DC, TOK], F32R)
        h16 = sb("h16", [P, 2, TOK], F16)
        hid = sb("hid", [P, RING, TOK], F32R)
        e16 = sb("e16", [P, TT, D], F16)

        turn_ps = pb("turn_ps", [P, 2, 2 * D], F16)
        up_ps = [pb(f"up{n}", [P, TOK]) for n in range(2)]
        down_ps = [pb(f"down{n}", [P, D]) for n in range(TT)]

        biases_in, w_in, w_hi, w_lo = sem("biases_in"), [sem("w_in0"), sem("w_in1")], sem("w_hi"), sem("w_lo")
        ident_set, ident16_set, rstd_ready = sem("ident_set"), sem("ident16_set"), sem("rstd_ready")
        x_loaded, ln_step, var_ready, root_done, xn_ready = sem("x_loaded"), sem("ln_step"), sem("var_ready"), sem("root_done"), sem("xn_ready")
        t_ready, xt_ready = sem("t_ready"), sem("xt_ready")
        up_ready, gelu_done, hid_ready, used = sem("up_ready"), sem("gelu_done"), sem("hid_ready"), sem("used")
        down_ready, e_ready, out_ready, stored = sem("down_ready"), sem("e_ready"), sem("out_ready"), sem("stored")
        block = es.enter_context(nc.Block())
        x_rows = x_in.rearrange("b s d -> (b s) d").rearrange("(n t p) d -> n p t d", t=TT, p=P)
        o_rows = x_out.rearrange("b s d -> (b s) d").rearrange("(n t p) d -> n p t d", t=TT, p=P)
        pieces = ([(w0s, c, w0[c * P:(c + 1) * P, :]) for c in range(DC)]
                  + [(w1s, g, w1[g * 4 * P:(g + 1) * 4 * P, :]) for g in range(FC // 4)])

        def part_of(w, k, hi):
            return w[hi][:, k, :] if w is w0s else w[hi][:, 4 * k:4 * k + 4, :].rearrange("p g n -> p (g n)")

        def steps(engine, step):
            step(0)
            with engine.Fori(1, N) as i:
                step(i)

        @block.sync
        def _(sp):
            sp.dma_start(x_tile[:, :, :], x_rows[0]).then_inc(x_loaded, 16)
            for n, (w, k, src) in enumerate(pieces):
                wait(sp, w_lo, n - 1)
                dst = stage[:, n % 2, :] if w is w0s else stage[:, n % 2, :].rearrange("p (g n) -> p g n", g=4)
                sp.dma_start(dst, src if w is w0s else src.rearrange("(g p) n -> p g n", p=P)).then_inc(w_in[n % 2], 16)
            sp.dma_start(bias0[:, :], b0).then_inc(biases_in, 16)
            sp.dma_start(bias1[:, :], b1.partition_broadcast(P)).then_inc(biases_in, 16)

            def step(i):
                if not isinstance(i, int):
                    sp.wait_ge(stored, 16 * i)
                    sp.dma_start(x_tile[:, :, :], x_rows[bass.ds(i, 1), :, :, :].rearrange("a p t d -> (a p) t d")).then_inc(x_loaded, 16)
                wait(sp, out_ready, TT * (i + 1))
                dst = o_rows[0] if isinstance(i, int) else o_rows[bass.ds(i, 1), :, :, :].rearrange("a p t d -> (a p) t d")
                sp.dma_start(dst, x_tile[:, :, :]).then_inc(stored, 16)

            steps(sp, step)
            sp.wait_ge(stored, 16 * N)

        @block.gpsimd
        def _(pool):
            pool.memset(ident[:, :], 0.0).then_inc(ident_set, 1)
            pool.wait_ge(ident_set, 1)
            pool.affine_select(out=ident[:, :], in_=ident[:, :], compare_op=ALU.not_equal, fill=1.0, base=0,
                               pattern=[[-1, P]], channel_multiplier=1).then_inc(ident_set, 1)

            def step(i):
                for t in range(TT):
                    wait(pool, e_ready, TT * i + t + 1)
                    pool.tensor_tensor(x_tile[:, t, :], x_tile[:, t, :], e16[:, t, :], ALU.add).then_inc(out_ready, 1)

            steps(pool, step)

        @block.scalar
        def _(act):
            for n, (w, k, _) in enumerate(pieces):
                act.wait_ge(w_in[n % 2], 16 * (n // 2 + 1))
                act.activation(part_of(w, k, 0), stage[:, n % 2, :], ACT.Copy).then_inc(w_hi, 1)
            act.wait_ge(biases_in, 32)

            def step(i):
                wait(act, var_ready, i + 1)
                act.activation(root[:, :], veps[:, :], ACT.Sqrt).then_inc(root_done, 1)
                for t in range(TT):
                    wait(act, t_ready, TT * i + t + 1)
                    act.activation(xt[:, :, t * P:(t + 1) * P], turn_ps[:, t % 2, 0:D].rearrange("p (c q) -> p c q", c=DC), ACT.Copy).then_inc(xt_ready, 1)
                for f in range(FC):
                    wait(act, up_ready, FC * i + f + 1)
                    wait(act, hid_ready, FC * i + f - 1)
                    act.activation(h16[:, f % 2, :], up_ps[f % 2][:, :], ACT.Gelu, bias=bias0[:, f:f + 1]).then_inc(gelu_done, 1)

            steps(act, step)

        @block.vector
        def _(dve):
            for n, (w, k, _) in enumerate(pieces):
                dve.wait_ge(w_hi, n + 1)
                dve.tensor_tensor(part_of(w, k, 1), stage[:, n % 2, :], part_of(w, k, 0).bitcast(F32), ALU.subtract).then_inc(w_lo, 1)
            dve.wait_ge(ident_set, 2)
            dve.tensor_copy(ident16[:, :], ident[:, :]).then_inc(ident16_set, 1)
            dve.wait_ge(biases_in, 32)

            def step(i):
                wait(dve, x_loaded, 16 * (i + 1))
                for t in range(TT):
                    dve.bn_stats(stats[:, t, :], x_tile[:, t, :]).then_inc(ln_step, 1)
                base = i * (2 * TT + 4)
                wait(dve, ln_step, base + TT)
                dve.memset(gate[:, :], 0.0)
                for t in range(TT):
                    dve.bn_aggr(mv[:, t, :], stats[:, t, :]).then_inc(ln_step, 1)
                base = base + 2 * TT
                wait(dve, ln_step, base)
                dve.tensor_scalar(veps[:, :], mv[:, :, 1], EPS, None, ALU.add).then_inc(var_ready, 1)
                wait(dve, root_done, i + 1)
                dve.reciprocal(r0[:, :], root[:, :]).then_inc(ln_step, 1)
                wait(dve, ln_step, base + 1)
                dve.tensor_tensor(r1[:, :], r0[:, :], r0[:, :], ALU.mult).then_inc(ln_step, 1)
                wait(dve, ln_step, base + 2)
                dve.tensor_tensor(r2[:, :], r1[:, :], veps[:, :], ALU.mult).then_inc(ln_step, 1)
                wait(dve, ln_step, base + 3)
                dve.tensor_scalar(r1[:, :], r2[:, :], -0.5, 1.5, ALU.mult, ALU.add).then_inc(ln_step, 1)
                wait(dve, ln_step, base + 4)
                dve.tensor_tensor(rstd[:, :], r1[:, :], r0[:, :], ALU.mult).then_inc(rstd_ready, 1)
                wait(dve, rstd_ready, i + 1)
                wait(dve, t_ready, TT * i)
                for t in range(TT):
                    dve.tensor_scalar(xn[:, t, :], x_tile[:, t, :], mv[:, t, 0:1], rstd[:, t:t + 1], ALU.subtract, ALU.mult).then_inc(xn_ready, 1)
                for f in range(FC):
                    wait(dve, gelu_done, FC * i + f + 1)
                    wait(dve, used, FC * i + f - RING + 1)
                    dve.tensor_copy(hid[:, f % RING, :], h16[:, f % 2, :]).then_inc(hid_ready, 1)
                wait(dve, out_ready, TT * i)
                for t in range(TT):
                    wait(dve, down_ready, i + 1)
                    dve.tensor_tensor(e16[:, t, :], down_ps[t][:, :], bias1[:, :], ALU.add).then_inc(e_ready, 1)

            steps(dve, step)

        @block.tensor
        def _(pe):
            pe.wait_ge(ident16_set, 1)
            pe.wait_ge(w_lo, len(pieces))

            def step(i):
                for t in range(TT):
                    wait(pe, xn_ready, TT * i + t + 1)
                    wait(pe, xt_ready, TT * i + t - 1)
                    for c in range(DC):
                        mm = pe.transpose(turn_ps[:, t % 2, c * P:(c + 1) * P], xn[:, t, c * P:(c + 1) * P], ident16[:, :])
                    mm.then_inc(t_ready, 1)
                wait(pe, xt_ready, TT * (i + 1))
                for f in range(FC + LAG):
                    if f < FC:
                        wait(pe, gelu_done, FC * i + f - 1)
                        for k in range(DC):
                            for h in range(2):
                                mm = pe.matmul(up_ps[f % 2][:, :], w0s[h][:, k, f * P:(f + 1) * P], xt[:, k, :],
                                               start=(k == 0 and h == 0), stop=(k == DC - 1 and h == 1))
                        mm.then_inc(up_ready, 1)
                    g = f - LAG
                    if g >= 0:
                        wait(pe, hid_ready, FC * i + g + 1)
                        if g == 0:
                            wait(pe, e_ready, TT * i)
                        for t in range(TT):
                            for h in range(2):
                                mm = pe.matmul(down_ps[t][:, :], hid[:, g % RING, t * P:(t + 1) * P], w1s[h][:, g, :],
                                               start=(g == 0 and h == 0), stop=(g == FC - 1 and h == 1))
                        mm.then_inc(used, 1)
                wait(pe, used, FC * (i + 1))
                pe.nop().then_inc(down_ready, 1)

            steps(pe, step)


def build(nc, a, out):
    B = a["x"].shape[0]
    x1 = nc.dram_tensor("x_after_self", a["x"].shape, F32, kind="Internal").ap()
    x2 = nc.dram_tensor("x_after_cross", a["x"].shape, F32, kind="Internal").ap()
    build_attention(nc, Attention("self", 32, True), B, a["x"], x1,
                    dict(q=a["self_wq"], kv=a["self_wkv"], o=a["self_wo"], bq=a["self_bq"], bk=a["self_bk"], bv=a["self_bv"], bo=a["self_bo"]))
    build_attention(nc, Attention("cross", 16, False), B, x1, x2,
                    dict(q=a["cross_wq"], kv=a["cross_wkv"], o=a["cross_wo"], bq=a["cross_bq"], bk=a["cross_bk"], bv=a["cross_bv"], bo=a["cross_bo"]),
                    ctx_t=a["ctx_t"], mask=a["mask"], mask_t=a["mask_t"], pad=a["pad"], pad_col=a["pad_col"])
    build_ffn(nc, B, x2, out, a["w0"], a["b0"], a["w1"], a["b1"])


def kernel(**inputs):
    import numpy as np
    import concourse.bacc as bacc
    from concourse.bass_utils import run_bass_kernel_spmd

    i = {k: np.asarray(v) for k, v in inputs.items()}
    order = np.arange(512).reshape(8, 4, 16).transpose(1, 0, 2).reshape(512)
    wqkv, bqkv = i["L0_attn_Wqkv_w"], i["L0_attn_Wqkv_b"]
    lay = {
        "x": i["x"],
        "self_wq": wqkv[:512].T, "self_wkv": np.concatenate([np.tile(wqkv[512:544].T, (1, 4)), wqkv[544:].T], 1),
        "self_wo": i["L0_attn_out_w"].T,
        "self_bq": bqkv[:512].reshape(4, 128).T, "self_bk": np.tile(bqkv[512:544], 4).reshape(128, 1),
        "self_bv": bqkv[544:], "self_bo": i["L0_attn_out_b"],
        "cross_wq": i["L0_xattn_Wq"].T[:, order], "cross_wkv": np.concatenate([i["L0_xattn_Wk"].T, i["L0_xattn_Wv"].T], 1),
        "cross_wo": i["L0_xattn_Wo"].T[order],
        "cross_bq": i["L0_xattn_bq"][order].reshape(4, 128).T, "cross_bk": i["L0_xattn_bk"].reshape(128, 1),
        "cross_bv": i["L0_xattn_bv"], "cross_bo": i["L0_xattn_bo"],
        "ctx_t": i["ctx_2048"].transpose(0, 2, 1),
        "mask": i["mask_SxS2_bc0"].view(np.uint32), "mask_t": np.ascontiguousarray(i["mask_SxS2_bc0"].T).view(np.uint32),
        "pad": i["mask_BxS2_bk0"].view(np.uint32),
        "pad_col": np.ascontiguousarray(i["mask_BxS2_bk0"].reshape(32, 128).T).view(np.uint32),
        "w0": i["L0_ffn_W0"].T, "b0": i["L0_ffn_bias0"].reshape(16, 128).T,
        "w1": i["L0_ffn_W1"].T, "b1": i["L0_ffn_bias1"],
    }
    nc = bacc.Bacc("TRN2", target_bir_lowering=False, num_devices=1)
    arrays, aps = {}, {}
    for name, v in lay.items():
        v = np.ascontiguousarray(v)
        arrays[f"in_{name}"] = v
        aps[name] = nc.dram_tensor(f"in_{name}", v.shape, mybir.dt.from_np(v.dtype), kind="ExternalInput").ap()
    out = nc.dram_tensor("out_x", i["x"].shape, F32, kind="ExternalOutput").ap()
    build(nc, aps, out)
    r = run_bass_kernel_spmd(nc, [arrays], core_ids=[0])
    return r.results[0]["out_x"]
```

```python
from contextlib import ExitStack

import concourse.bass as bass
from concourse import mybir

ALU = mybir.AluOpType
ACT = mybir.ActivationFunctionType
AX = mybir.AxisListType
F32 = mybir.dt.float32
F32R = mybir.dt.float32r
BF16 = mybir.dt.bfloat16
F16 = mybir.dt.float16
U32 = mybir.dt.uint32
U8 = mybir.dt.uint8

P = 128
D = 512
DC = D // P
S = 256
NT = S // P
BIG = 1e30
SHIFT_MAX = 1e29
EPS = 1e-5
STACK = 97


class Attention:

    def __init__(self, name, head_dim, causal):
        self.name = name
        self.HD = head_dim
        self.NB = P // head_dim
        self.NH = self.NB * DC
        self.causal = causal
        self.KB = 1 if causal else self.NB
        self.VD = head_dim * self.KB
        self.scale = float(head_dim) ** -0.5
        self.shift_row = 3 * head_dim
        self.max_units = []
        for qt in range(NT):
            width = P * (qt + 1) if causal else S
            n = 512 // width
            self.max_units += [(qt, c, b, n, width) for c in range(DC) for b in range(0, self.NB, n)]
        self.groups = []
        halves = self.NB // 4
        for qt in range(NT):
            key_tiles = range(qt + 1) if causal else range(NT)
            for half in range(halves):
                blocks = [halves * j + half for j in range(4)]
                for kt in key_tiles:
                    first, last = (half, kt) == (0, 0), (half, kt) == (halves - 1, key_tiles[-1])
                    self.groups.append((qt, half, blocks, kt, first, last))
        self.NG = len(self.groups)
        self.NU = 4 * self.NG
        assert self.NU == len(self.max_units)
        self.groups_of_tile0 = sum(g[0] == 0 for g in self.groups)
        self.max_units_of_tile0 = sum(u[0] == 0 for u in self.max_units)
        if causal:
            self.pe_plan = {1: ["shift1"], 3: ["out1"], 5: ["t0"], 6: ["t1"], 7: ["k"], 8: ["v", "q0"], 9: ["q1"], 10: ["shift0"], 11: ["out0"]}
            self.act_plan = {1: ["guess"], 2: ["shift1"], 3: ["head1"], 6: ["t0"], 7: ["t1"], 8: ["k"], 9: ["head0", "q0"], 10: ["q1"], 11: ["shift0"]}
            self.dve_plan = {0: ["stats"], 2: ["recip1", "head1", "v_use"], 3: ["apply", "out1"], 6: ["t0"], 7: ["t1", "recip0"], 8: ["k"],
                             9: ["v", "head0", "q0"], 10: ["q1"], 11: ["out0"]}
        else:
            self.pe_plan = {2: ["shift1"], 8: ["out1"], 10: ["k"], 11: ["v"], 14: ["t0"], 16: ["t1"], 18: ["q0"], 20: ["q1"], 22: ["shift0"], 26: ["out0"]}
            self.act_plan = {1: ["src"], 3: ["shift1"], 5: ["guess"], 6: ["head1"], 11: ["k"], 15: ["t0"], 17: ["t1"], 19: ["q0"], 21: ["q1"],
                             23: ["shift0"], 24: ["head0"]}
            self.dve_plan = {1: ["stats"], 2: ["src"], 3: ["recip1"], 4: ["v_use"], 7: ["head1"], 8: ["apply"], 9: ["out1"], 11: ["k"], 13: ["v"],
                             15: ["t0"], 17: ["t1"], 18: ["recip0"], 20: ["q0"], 22: ["q1"], 25: ["head0"], 28: ["out0"]}


def wait(engine, sem, value):
    if isinstance(value, int) and value <= 0:
        return
    engine.wait_ge(sem, value)


def spread(ap, times):
    return ap.unsqueeze(1).broadcast_to([ap.shape[0], times, ap.shape[1]])


def build_attention(nc, A, B, x_in, x_out, w, ctx_t=None, mask=None, mask_t=None, pad=None, pad_col=None):
    HD, NB, KB, VD, NH, NG, NU = A.HD, A.NB, A.KB, A.VD, A.NH, A.NG, A.NU
    cross = not A.causal
    with ExitStack() as es:
        def sb(name, shape, dt):
            return es.enter_context(nc.sbuf_tensor(f"{A.name}_{name}", shape, dt))

        def pb(name, shape, dt=F32):
            return es.enter_context(nc.psum_tensor(f"{A.name}_{name}", shape, dt))

        def sem(name):
            return es.enter_context(nc.semaphore(f"{A.name}_{name}"))

        wq = [sb(f"wq{n}", [P, DC, D], F32R) for n in range(2)]
        wkv = [sb(f"wkv{n}", [P, DC, P + VD], F32R) for n in range(2)]
        wo = [sb(f"wo{n}", [P, DC, D], F32R) for n in range(2)]
        bq = sb("bq", [P, DC], F32)
        bk = sb("bk", [P, 1], F32)
        bv = sb("bv", [P, VD], F32)
        bo = sb("bo", [P, D], F32)
        ident = sb("ident", [P, P], F32)
        ident16 = sb("ident16", [P, P], BF16)
        block_mask = sb("block_mask", [P, NB], F32)
        ones_v = sb("ones_v", [P, 2, 32], F32)
        ones_row = sb("ones_row", [1, S], F32R)
        mask_q0 = sb("mask_q0", [P, NT, S], BF16)
        mask_k0 = sb("mask_k0", [P, NT, S], BF16)
        x_tile = sb("x_tile", [P, NT, D], F32)
        stats = sb("stats", [P, NT, 6], F32)
        mv = sb("mv", [P, NT, 2], F32)
        veps = sb("veps", [P, NT], F32)
        lnv = sb("lnv", [P, NT], F32)
        r0 = sb("r0", [P, NT], F32)
        r1 = sb("r1", [P, NT], F32)
        r2 = sb("r2", [P, NT], F32)
        gate = sb("gate", [P, 1], F32)
        rstd = sb("rstd", [P, NT], F32)
        xt = [sb(f"xt{n}", [P, DC, S], F32R) for n in range(2)]
        q_parts = [[sb(f"q{m}{n}", [P, DC, S], F32R) for n in range(2)] for m in range(2)]
        k_parts = [sb(f"k{n}", [P, S], F32R) for n in range(2)]
        k_blocks = [sb(f"k_blocks{m}", [P, NB, S], F32R) for m in range(2)]
        v_new = sb("v_new", [P, NT, VD], F32)
        v_use = [sb(f"v_use{m}", [P, NT, KB, 32], F32) for m in range(2)]
        row_max = sb("row_max", [P, NT, NB, DC], F32)
        shift = sb("shift", [P, NT, NH], F32)
        shift_t = sb("shift_t", [NH, NT, P], F32R)
        q_stack = sb("q_stack", [STACK, NT, NB * DC, P], F32R)
        k_stack = [sb(f"k_stack{m}", [STACK, KB, S], F32R) for m in range(2)]
        probs = sb("probs", [P, 2, 4, 512], F32)
        recip = sb("recip", [P, 512], F32)
        heads = sb("heads", [P, NT, 512], F32)
        ht = [sb(f"ht{n}", [P, NT, DC, P], F32R) for n in range(2)]
        x_res = sb("x_res", [P, NT, D], F32)
        if cross:
            src = sb("src", [P, DC, S], F32)
            mask_words = sb("mask_words", [P, 2, NT, S // 4], U32)
            pad_words = sb("pad_words", [P, S // 4], U32)
            pad_f = sb("pad_f", [P, S], F32)
            padc_words = sb("padc_words", [P, B * NT // 4], U32)
            padc_f = sb("padc_f", [P, B * NT], F32)
            mask_q = [sb(f"mask_q_of{m}", [P, NT, S], BF16) for m in range(2)]
            mask_k = [sb(f"mask_k_of{m}", [P, NT, S], BF16) for m in range(2)]
        else:
            mask_q, mask_k = [mask_q0] * 2, [mask_k0] * 2
        staged = probs[:, :, :, :].rearrange("p a b n -> p (a b n)")
        stages = [(wq, D, staged[:, 0:DC * D]), (wkv, P + VD, staged[:, DC * D:DC * (D + P + VD)]), (wo, D, staged[:, 0:DC * D])]
        stages = [(part, st.rearrange("p (c n) -> p c n", c=DC)) for part, _, st in stages]

        proj = [pb(f"proj{n}", [P, 512]) for n in range(2)]
        max_ps = [pb(f"max{n}", [P, 512]) for n in range(2)]
        score_ps = [pb(f"score{n}", [P, 512]) for n in range(2)]
        heads_ps = pb("heads_ps", [P, 512])
        sums_ps = pb("sums_ps", [P, 512])
        shift_rows = nc.dram_tensor(f"{A.name}_shift_rows", [NT, NH, P], F32, kind="Internal").ap()

        biases_in, masks_in, ones_in = sem("biases_in"), sem("masks_in"), sem("ones_in")
        w_in, w_hi, w_lo = [sem(f"w_in{n}") for n in range(3)], sem("w_hi"), sem("w_lo")
        ident_set, masks_set, consts_set, stacks_set = sem("ident_set"), sem("masks_set"), sem("consts_set"), sem("stacks_set")
        x_loaded, src_loaded, pad_loaded = sem("x_loaded"), sem("src_loaded"), sem("pad_loaded")
        ln_step, var_ready, ln_done, rsqrt_done, xn_ready = sem("ln_step"), sem("var_ready"), sem("ln_done"), sem("rsqrt_done"), sem("xn_ready")
        t_ready, xt_hi, xt_lo = sem("t_ready"), sem("xt_hi"), sem("xt_lo")
        src_hi, src_lo = sem("src_hi"), sem("src_lo")
        q_ready, q_hi, q_lo = sem("q_ready"), sem("q_hi"), sem("q_lo")
        k_ready, k_hi, k_lo, kb_ready = sem("k_ready"), sem("k_hi"), sem("k_lo"), sem("kb_ready")
        v_ready, v_done = sem("v_ready"), sem("v_done")
        padf_set, mask_q_ready, mask_k_ready = sem("padf_set"), sem("mask_q_ready"), sem("mask_k_ready")
        max_ready, max_done, shift_ready, shift_t_ready, shift_t_done = (
            sem("max_ready"), sem("max_done"), sem("shift_ready"), sem("shift_t_ready"), sem("shift_t_done"))
        k_stacked, v_use_ready = sem("k_stacked"), sem("v_use_ready")
        q_stacked, shift_spilled, shift_stacked = ([sem(f"{n}{t}") for t in range(NT)] for n in ("q_stacked", "shift_spilled", "shift_stacked"))
        score_ready, exp_done, pv_done = sem("score_ready"), sem("exp_done"), sem("pv_done")
        recip_done, heads_ready, ht_hi, ht_lo = sem("recip_done"), sem("heads_ready"), sem("ht_hi"), sem("ht_lo")
        res_biased, o_ready, o_done = sem("res_biased"), sem("o_ready"), sem("o_done")
        res_loaded, stored = ([sem(f"{n}{t}") for t in range(NT)] for n in ("res_loaded", "stored"))
        block = es.enter_context(nc.Block())

        def rows(dram, i, t):
            return dram[bass.ds(i, 1), t * P:(t + 1) * P, :].rearrange("a p d -> (a p) d")

        def has(m):
            return not isinstance(m, int) or 0 <= m < B

        def steps(engine, step):
            for i in (-1, 0, 1, 2):
                step(i, i % 2)
            with engine.Fori(3, B - 2, 2) as i:
                step(i, 1)
                step(i + 1, 0)
            for i in (B - 1, B, B + 1):
                step(i, i % 2)

        @block.sync
        def _(sp):
            def load_weights(n, dram):
                sp.dma_start(stages[n][1], dram.rearrange("(c p) n -> p c n", p=P)).then_inc(w_in[n], 16)

            load_weights(0, w["q"])
            load_weights(1, w["kv"])
            sp.dma_start(bq[:, :], w["bq"]).then_inc(biases_in, 16)
            sp.dma_start(bk[:, :], w["bk"]).then_inc(biases_in, 16)
            sp.dma_start(bv[:, :], w["bv"].partition_broadcast(P)).then_inc(biases_in, 16)
            sp.dma_start(bo[:, :], w["bo"].partition_broadcast(P)).then_inc(biases_in, 16)
            if cross:
                sp.dma_start(mask_words[:, 0], mask.rearrange("(t p) k -> p t k", p=P)).then_inc(masks_in, 16)
                sp.dma_start(mask_words[:, 1], mask_t.rearrange("(t p) q -> p t q", p=P)).then_inc(masks_in, 16)
                sp.dma_start(padc_words[:, :], pad_col).then_inc(masks_in, 16)
            sp.wait_ge(w_lo, 1)
            load_weights(2, w["o"])
            sp.wait_ge(stacks_set, 4)
            for m in range(2):
                for g in range(KB):
                    sp.dma_start(k_stack[m][A.shift_row:A.shift_row + 1, g, :].bitcast(F32), ones_row[0:1, :].bitcast(F32)).then_inc(ones_in, 16)

            def stack_q(m, par, t):
                for part, at in ((0, 0), (1, 1), (0, 2)):
                    for g in range(NB):
                        sp.dma_start(q_stack[at * HD:(at + 1) * HD, t, g * DC:(g + 1) * DC, :].bitcast(F32),
                                     q_parts[par][part][g * HD:(g + 1) * HD, :, t * P:(t + 1) * P].bitcast(F32)).then_inc(q_stacked[t], 16)

            def stack_shift(m, t):
                wait(sp, shift_t_done, NT * m + t + 1)
                sp.dma_start(shift_rows[t], shift_t[:, t, :].bitcast(F32)).then_inc(shift_spilled[t], 16)
                wait(sp, shift_spilled[t], 16 * (m + 1))
                sp.dma_start(q_stack[A.shift_row:A.shift_row + 1, t, 0:NH, :].bitcast(F32), shift_rows[t:t + 1]).then_inc(shift_stacked[t], 16)

            def step(i, par):
                n = i + 1
                if has(n):
                    wait(sp, t_ready, NT * n)
                    for t in range(NT):
                        sp.dma_start(x_tile[:, t, :], rows(x_in, n, t)).then_inc(x_loaded, 16)
                    if cross:
                        wait(sp, src_lo, n)
                        sp.dma_start(src[:, :, :], ctx_t[bass.ds(n, 1), :, :].rearrange("a (c p) s -> p (a c) s", p=P)).then_inc(src_loaded, 16)
                        wait(sp, padf_set, n)
                        sp.dma_start(pad_words[:, :], pad[bass.ds(n, 1), :].rearrange("a s -> (a s)").partition_broadcast(P)).then_inc(pad_loaded, 16)
                if has(i - 1):
                    wait(sp, score_ready, NU * (i - 1))
                    stack_q(i - 1, 1 - par, 1)
                if has(i):
                    wait(sp, k_lo, i + 1)
                    if not has(i - 1):
                        wait(sp, ones_in, 32 * KB)
                    else:
                        wait(sp, score_ready, NU * (i - 1))
                    for part, at in ((0, 0), (0, 1), (1, 2)):
                        for g in range(KB):
                            sp.dma_start(k_stack[par][at * HD:(at + 1) * HD, g, :].bitcast(F32),
                                         k_parts[part][g * HD:(g + 1) * HD, :].bitcast(F32)).then_inc(k_stacked, 16)
                if has(i - 1):
                    stack_shift(i - 1, 1)
                    wait(sp, stored[0], 16 * (i - 1))
                    sp.dma_start(x_res[:, 0, :], rows(x_in, i - 1, 0)).then_inc(res_loaded[0], 16)
                if has(i - 2):
                    wait(sp, o_done, NT * (i - 2) + 2)
                    sp.dma_start(rows(x_out, i - 2, 1), x_res[:, 1, :]).then_inc(stored[1], 16)
                if has(i - 1):
                    wait(sp, stored[1], 16 * (i - 1))
                    sp.dma_start(x_res[:, 1, :], rows(x_in, i - 1, 1)).then_inc(res_loaded[1], 16)
                if has(i):
                    wait(sp, q_lo, DC * (i + 1))
                    if has(i - 1):
                        wait(sp, score_ready, NU * i + (4 * A.groups_of_tile0 - NU))
                    stack_q(i, par, 0)
                    stack_shift(i, 0)
                if has(i - 1):
                    wait(sp, o_done, NT * (i - 1) + 1)
                    sp.dma_start(rows(x_out, i - 1, 0), x_res[:, 0, :]).then_inc(stored[0], 16)

            steps(sp, step)
            for t in range(NT):
                sp.wait_ge(stored[t], 16 * B)

        @block.gpsimd
        def _(pool):
            pool.memset(ident[:, :], 0.0).then_inc(ident_set, 1)
            pool.memset(mask_q0[:, :, :], 0.0).then_inc(ident_set, 1)
            pool.memset(mask_k0[:, :, :], 0.0).then_inc(ident_set, 1)
            pool.memset(block_mask[:, :], 1.0).then_inc(ident_set, 1)
            pool.wait_ge(ident_set, 4)
            pool.affine_select(out=ident[:, :], in_=ident[:, :], compare_op=ALU.not_equal, fill=1.0, base=0,
                               pattern=[[-1, P]], channel_multiplier=1).then_inc(ident_set, 1)
            pool.affine_select(out=block_mask[:, :], in_=block_mask[:, :], compare_op=ALU.is_ge, fill=0.0, base=0,
                               pattern=[[-HD, NB]], channel_multiplier=1).then_inc(ident_set, 1)
            pool.wait_ge(ident_set, 6)
            pool.affine_select(out=block_mask[:, :], in_=block_mask[:, :], compare_op=ALU.is_ge, fill=0.0, base=HD - 1,
                               pattern=[[HD, NB]], channel_multiplier=-1).then_inc(ident_set, 1)
            if A.causal:
                pool.affine_select(out=mask_q0[:, :, :], in_=mask_q0[:, :, :], compare_op=ALU.is_ge, fill=-BIG, base=0,
                                   pattern=[[P, NT], [-1, S]], channel_multiplier=1).then_inc(masks_set, 1)
                pool.affine_select(out=mask_k0[:, :, :], in_=mask_k0[:, :, :], compare_op=ALU.is_ge, fill=-BIG, base=0,
                                   pattern=[[-P, NT], [1, S]], channel_multiplier=-1).then_inc(masks_set, 1)
            pool.wait_ge(biases_in, 64)

            def step(i, par):
                if has(i - 1):
                    for t in range(NT):
                        wait(pool, res_loaded[t], 16 * i)
                        pool.tensor_tensor(x_res[:, t, :], x_res[:, t, :], bo[:, :], ALU.add).then_inc(res_biased, 1)

            steps(pool, step)

        @block.scalar
        def _(act):
            for n, (part, st) in enumerate(stages):
                act.wait_ge(w_in[n], 16)
                act.activation(part[0][:, :, :], st, ACT.Copy).then_inc(w_hi, 1)
            act.wait_ge(biases_in, 64)
            act.wait_ge(w_lo, 3)

            def rsqrt_guess(n):
                wait(act, var_ready, n + 1)
                act.activation(lnv[:, :], veps[:, :], ACT.Ln).then_inc(ln_done, 1)
                wait(act, ln_done, n + 1)
                act.activation(r0[:, :], lnv[:, :], ACT.Exp, scale=-0.5).then_inc(rsqrt_done, 1)

            def src_high(n):
                wait(act, src_loaded, 16 * (n + 1))
                wait(act, q_ready, 2 * n)
                act.activation(xt[0][:, :, :], src[:, :, :], ACT.Copy).then_inc(src_hi, 1)

            def t_high(n, t):
                wait(act, t_ready, NT * n + t + 1)
                if cross:
                    wait(act, v_ready, n + 1)
                else:
                    wait(act, q_ready, 2 * n)
                act.activation(xt[0][:, :, t * P:(t + 1) * P], proj[t][:, :].rearrange("p (c q) -> p c q", c=DC), ACT.Copy).then_inc(xt_hi, 1)

            def q_high(n, par, half):
                wait(act, q_ready, 2 * n + half + 1)
                if half == 0:
                    for t in range(NT):
                        wait(act, q_stacked[t], 16 * 3 * NB * (n - 1))
                    wait(act, max_ready, NU * (n - 1))
                for c in (2 * half, 2 * half + 1):
                    act.activation(q_parts[par][0][:, c, :], proj[half][:, (c % 2) * S:(c % 2 + 1) * S], ACT.Identity, bias=bq[:, c:c + 1]).then_inc(q_hi, 1)

            def k_high(n):
                wait(act, k_ready, n + 1)
                wait(act, k_stacked, 16 * 3 * KB * n)
                act.activation(k_parts[0][:, :], proj[0][:, 0:S], ACT.Identity, bias=bk[:, 0:1]).then_inc(k_hi, 1)

            def shift_copy(m, t):
                wait(act, shift_t_ready, NT * m + t + 1)
                wait(act, shift_spilled[t], 16 * m)
                act.activation(shift_t[:, t, :], proj[0][0:NH, 0:P], ACT.Copy).then_inc(shift_t_done, 1)

            def head_high(m, t):
                wait(act, heads_ready, NT * m + t + 1)
                wait(act, o_ready, NT * (m - 1) + t + 1)
                act.activation(ht[0][:, t, :, :], heads[:, t, :].rearrange("p (c q) -> p c q", c=DC), ACT.Copy).then_inc(ht_hi, 1)

            def step(i, par):
                n, b = i + 1, i - 1
                jobs = {
                    "guess": (n, lambda: rsqrt_guess(n)), "src": (n, lambda: src_high(n)),
                    "t0": (n, lambda: t_high(n, 0)), "t1": (n, lambda: t_high(n, 1)),
                    "q0": (n, lambda: q_high(n, 1 - par, 0)), "q1": (n, lambda: q_high(n, 1 - par, 1)), "k": (n, lambda: k_high(n)),
                    "shift0": (i, lambda: shift_copy(i, 0)), "shift1": (i - 1, lambda: shift_copy(i - 1, 1)),
                    "head0": (i - 1, lambda: head_high(i - 1, 0)), "head1": (i - 2, lambda: head_high(i - 2, 1)),
                }
                for u in range(NU):
                    if has(b):
                        k = u // 4
                        half = (NG * (1 - par) + k) % 2
                        if u % 4 == 0:
                            wait(act, pv_done, NG * b + k - 1)
                        wait(act, score_ready, NU * b + u + 1)
                        act.activation(probs[:, half, u % 4, :], score_ps[u % 2][:, :], ACT.Exp, scale=A.scale).then_inc(exp_done, 1)
                    for job in A.act_plan.get(u, ()):
                        m, do = jobs[job]
                        if has(m):
                            do()

            steps(act, step)

        @block.vector
        def _(dve):
            for n, (part, st) in enumerate(stages):
                dve.wait_ge(w_hi, n + 1)
                dve.tensor_tensor(part[1][:, :, :], st, part[0][:, :, :].bitcast(F32), ALU.subtract).then_inc(w_lo, 1)
                if n == 1:
                    dve.memset(q_stack[:, :, :, :].bitcast(F32), 0.0).then_inc(stacks_set, 1)
                    for m in range(2):
                        dve.memset(k_stack[m][:, :, :].bitcast(F32), 0.0).then_inc(stacks_set, 1)
                    dve.memset(ones_row[:, :].bitcast(F32), 1.0).then_inc(stacks_set, 1)
            for m in range(2):
                dve.memset(v_use[m][:, :, :, :], 0.0).then_inc(consts_set, 1)
            if cross:
                dve.memset(ones_v[:, :, :], 0.0).then_inc(consts_set, 1)
                dve.wait_ge(consts_set, 3)
                dve.memset(ones_v[:, 0, 0:HD], 1.0).then_inc(consts_set, 1)
                dve.memset(ones_v[:, 1, HD:2 * HD], 1.0).then_inc(consts_set, 1)
                dve.wait_ge(masks_in, 48)
                dve.wait_ge(ident_set, 7)
                dve.tensor_scalar(mask_q0[:, :, :], mask_words[:, 0].bitcast(U8), -BIG, None, ALU.mult).then_inc(consts_set, 1)
                dve.tensor_scalar(mask_k0[:, :, :], mask_words[:, 1].bitcast(U8), -BIG, None, ALU.mult).then_inc(consts_set, 1)
                dve.tensor_scalar(padc_f[:, :], padc_words[:, :].bitcast(U8), -BIG, None, ALU.mult).then_inc(consts_set, 1)
            else:
                dve.memset(ones_v[:, :, :], 1.0).then_inc(consts_set, 1)
            dve.wait_ge(ident_set, 7)
            dve.tensor_copy(ident16[:, :], ident[:, :]).then_inc(consts_set, 1)
            dve.wait_ge(consts_set, (9 if cross else 4))
            dve.wait_ge(biases_in, 64)

            def norm_stats(n):
                wait(dve, x_loaded, 16 * NT * (n + 1))
                for t in range(NT):
                    dve.bn_stats(stats[:, t, :], x_tile[:, t, :]).then_inc(ln_step, 1)
                wait(dve, ln_step, 8 * n + 2)
                dve.memset(gate[:, :], 0.0)
                for t in range(NT):
                    dve.bn_aggr(mv[:, t, :], stats[:, t, :]).then_inc(ln_step, 1)
                wait(dve, ln_step, 8 * n + 4)
                dve.tensor_scalar(veps[:, :], mv[:, :, 1], EPS, None, ALU.add).then_inc(var_ready, 1)

            def norm_apply(n):
                wait(dve, rsqrt_done, n + 1)
                dve.tensor_tensor(r1[:, :], r0[:, :], r0[:, :], ALU.mult).then_inc(ln_step, 1)
                wait(dve, ln_step, 8 * n + 5)
                dve.tensor_tensor(r2[:, :], r1[:, :], veps[:, :], ALU.mult).then_inc(ln_step, 1)
                wait(dve, ln_step, 8 * n + 6)
                dve.tensor_scalar(r1[:, :], r2[:, :], -0.5, 1.5, ALU.mult, ALU.add).then_inc(ln_step, 1)
                wait(dve, ln_step, 8 * n + 7)
                dve.tensor_tensor(rstd[:, :], r1[:, :], r0[:, :], ALU.mult).then_inc(ln_step, 1)
                wait(dve, ln_step, 8 * n + 8)
                for t in range(NT):
                    dve.tensor_scalar(x_tile[:, t, :], x_tile[:, t, :], mv[:, t, 0:1], rstd[:, t:t + 1], ALU.subtract, ALU.mult).then_inc(xn_ready, 1)

            def src_low(n):
                wait(dve, src_hi, n + 1)
                dve.tensor_tensor(xt[1][:, :, :], src[:, :, :], xt[0][:, :, :].bitcast(F32), ALU.subtract).then_inc(src_lo, 1)

            def t_low(n, t):
                wait(dve, xt_hi, NT * n + t + 1)
                dve.tensor_tensor(xt[1][:, :, t * P:(t + 1) * P], proj[t][:, :].rearrange("p (c q) -> p c q", c=DC),
                                  xt[0][:, :, t * P:(t + 1) * P].bitcast(F32), ALU.subtract).then_inc(xt_lo, 1)

            def q_low(n, par, half):
                wait(dve, q_hi, DC * n + 2 * half + 2)
                for c in (2 * half, 2 * half + 1):
                    dve.scalar_tensor_tensor(out=q_parts[par][1][:, c, :], in0=proj[half][:, (c % 2) * S:(c % 2 + 1) * S], scalar=bq[:, c:c + 1],
                                             in1=q_parts[par][0][:, c, :].bitcast(F32), op0=ALU.add, op1=ALU.subtract).then_inc(q_lo, 1)

            def k_low(n, par):
                wait(dve, k_hi, n + 1)
                dve.scalar_tensor_tensor(out=k_parts[1][:, :], in0=proj[0][:, 0:S], scalar=bk[:, 0:1],
                                         in1=k_parts[0][:, :].bitcast(F32), op0=ALU.add, op1=ALU.subtract).then_inc(k_lo, 1)
                wait(dve, max_ready, NU * (n - 1))
                dve.tensor_tensor(k_blocks[par][:, :, :], spread(k_parts[0][:, :].bitcast(F32), NB),
                                  block_mask[:, :].unsqueeze(2).broadcast_to([P, NB, S]), ALU.mult).then_inc(kb_ready, 1)

            def v_and_mask(n, par):
                wait(dve, v_ready, n + 1)
                dve.tensor_tensor(v_new[:, :, :], proj[1][:, 0:NT * VD].rearrange("p (t v) -> p t v", t=NT), spread(bv[:, :], NT), ALU.add).then_inc(v_done, 1)
                if cross:
                    wait(dve, pad_loaded, 16 * (n + 1))
                    dve.tensor_scalar(pad_f[:, :], pad_words[:, :].bitcast(U8), -BIG, None, ALU.mult).then_inc(padf_set, 1)
                    wait(dve, padf_set, n + 1)
                    wait(dve, max_ready, NU * (n - 1))
                    dve.tensor_tensor(mask_q[par][:, :, :], mask_q0[:, :, :], spread(pad_f[:, :], NT), ALU.add).then_inc(mask_q_ready, 1)

            def v_and_mask_for_use(m, par):
                wait(dve, pv_done, NG * (m - 1))
                wait(dve, v_done, m + 1)
                if A.causal:
                    dve.tensor_copy(v_use[par][:, :, 0, :], v_new[:, :, :]).then_inc(v_use_ready, 1)
                else:
                    for half in range(2):
                        dve.tensor_copy(v_use[par][:, :, half:NB:2, half * HD:(half + 1) * HD],
                                        v_new[:, :, :].rearrange("p t (j h d) -> p t j h d", h=2, d=HD)[:, :, :, half, :]).then_inc(v_use_ready, 1)
                    wait(dve, score_ready, NU * (m - 1))
                    for kt in range(NT):
                        dve.tensor_scalar(mask_k[par][:, kt, :], mask_k0[:, kt, :], padc_f[:, bass.ds(m * NT + kt, 1)], None, ALU.add).then_inc(mask_k_ready, 1)

            def shifts(m, t):
                wait(dve, max_done, NU * m + (A.max_units_of_tile0 if t == 0 else NU))
                wait(dve, shift_t_ready, NT * (m - 1) + t + 1)
                dve.tensor_scalar(shift[:, t, :].rearrange("p (g c) -> p g c", c=DC), row_max[:, t, :, :], -1.0, SHIFT_MAX,
                                  ALU.mult, ALU.min).then_inc(shift_ready, 1)

            def normalise(m, t):
                wait(dve, pv_done, NG * m + (A.groups_of_tile0 if t == 0 else NG))
                dve.reciprocal(recip[:, :], sums_ps[:, :]).then_inc(recip_done, 1)
                wait(dve, recip_done, NT * m + t + 1)
                wait(dve, ht_hi, NT * (m - 1) + t + 1)
                dve.tensor_tensor(heads[:, t, :], heads_ps[:, :], recip[:, :], ALU.mult).then_inc(heads_ready, 1)

            def head_low(m, t):
                wait(dve, ht_hi, NT * m + t + 1)
                dve.tensor_tensor(ht[1][:, t, :, :].rearrange("p c q -> p (c q)"), heads[:, t, :],
                                  ht[0][:, t, :, :].rearrange("p c q -> p (c q)").bitcast(F32), ALU.subtract).then_inc(ht_lo, 1)

            def out_add(m, t):
                wait(dve, o_ready, NT * m + t + 1)
                wait(dve, res_biased, NT * m + t + 1)
                dve.tensor_tensor(x_res[:, t, :], proj[1][:, :], x_res[:, t, :], ALU.add).then_inc(o_done, 1)

            def step(i, par):
                n = i + 1
                jobs = {
                    "stats": (n, lambda: norm_stats(n)), "apply": (n, lambda: norm_apply(n)), "src": (n, lambda: src_low(n)),
                    "t0": (n, lambda: t_low(n, 0)), "t1": (n, lambda: t_low(n, 1)),
                    "q0": (n, lambda: q_low(n, 1 - par, 0)), "q1": (n, lambda: q_low(n, 1 - par, 1)),
                    "k": (n, lambda: k_low(n, 1 - par)), "v": (n, lambda: v_and_mask(n, 1 - par)),
                    "v_use": (i, lambda: v_and_mask_for_use(i, par)),
                    "recip0": (i - 1, lambda: normalise(i - 1, 0)), "recip1": (i - 2, lambda: normalise(i - 2, 1)),
                    "head0": (i - 1, lambda: head_low(i - 1, 0)), "head1": (i - 2, lambda: head_low(i - 2, 1)),
                    "out0": (i - 1, lambda: out_add(i - 1, 0)), "out1": (i - 2, lambda: out_add(i - 2, 1)),
                }
                for u, (qt, c, blk, nb, width) in enumerate(A.max_units):
                    if has(i):
                        wait(dve, max_ready, NU * i + u + 1)
                        dve.tensor_reduce(row_max[:, qt, blk:blk + nb, c], max_ps[u % 2][:, :].rearrange("p (b k) -> p b k", b=nb),
                                          AX.X, ALU.max).then_inc(max_done, 1)
                        if u == A.max_units_of_tile0 - 1:
                            shifts(i, 0)
                        if u == NU - 1:
                            shifts(i, 1)
                    for job in A.dve_plan.get(u, ()):
                        m, do = jobs[job]
                        if has(m):
                            do()

            steps(dve, step)

        @block.tensor
        def _(pe):
            pe.wait_ge(consts_set, (9 if cross else 4))
            if A.causal:
                pe.wait_ge(masks_set, 2)
            pe.wait_ge(w_lo, 3)

            def three(out, a, b, first, last):
                for k, (x, y) in enumerate(((0, 0), (1, 0), (0, 1))):
                    mm = pe.matmul(out, a[x], b[y], start=first and k == 0, stop=last and k == 2)
                return mm

            def max_unit(i, par, u):
                qt, c, blk, nb, width = A.max_units[u]
                if u == 0:
                    wait(pe, kb_ready, i + 1)
                    wait(pe, q_hi, DC * (i + 1))
                    if cross:
                        wait(pe, mask_q_ready, i + 1)
                wait(pe, max_done, NU * i + u - 1)
                out = max_ps[u % 2][:, :]
                pe.matmul(out, q_parts[par][0][:, c, qt * P:(qt + 1) * P], k_blocks[par][:, blk:blk + nb, 0:width], start=True, stop=False)
                pe.matmul(out, ident16[:, :], spread(mask_q[par][:, qt, 0:width], nb), start=False, stop=True).then_inc(max_ready, 1)

            def score_unit(b, par, u):
                qt, half, blocks, kt, first, last = A.groups[u // 4]
                g = blocks[u % 4]
                masked = cross or kt == qt
                if u == 0:
                    wait(pe, k_stacked, 16 * 3 * KB * (b + 1))
                    if cross:
                        wait(pe, mask_k_ready, NT * (b + 1))
                if u == 4 * A.groups_of_tile0 * qt:
                    wait(pe, q_stacked[qt], 16 * 3 * NB * (b + 1))
                    wait(pe, shift_stacked[qt], 16 * (b + 1))
                wait(pe, exp_done, NU * b + u - 1)
                out = score_ps[u % 2][:, :]
                mm = pe.matmul(out, k_stack[par][:, 0 if A.causal else g, kt * P:(kt + 1) * P],
                               q_stack[:, qt, g * DC:(g + 1) * DC, :], start=True, stop=not masked)
                if masked:
                    mm = pe.matmul(out, ident16[:, :], spread(mask_k[par][:, kt, qt * P:(qt + 1) * P], DC), start=False, stop=True)
                mm.then_inc(score_ready, 1)

            def pv_group(b, par, k):
                qt, half, blocks, kt, first, last = A.groups[k]
                wait(pe, exp_done, NU * b + 4 * (k + 1))
                if k == 0:
                    wait(pe, v_use_ready, (2 if cross else 1) * (b + 1))
                if first:
                    wait(pe, heads_ready, NT * b + qt)
                for out_ps, w_of in ((heads_ps, lambda g: v_use[par][:, kt, 0 if A.causal else g, :]), (sums_ps, lambda g: ones_v[:, half, :])):
                    for j, g in enumerate(blocks):
                        mm = pe.matmul(out_ps[32 * j:32 * j + 32, :], w_of(g), probs[:, (NG * par + k) % 2, j, :],
                                       start=first, stop=last, tile_position=(0, 32 * j))
                mm.then_inc(pv_done, 1)

            def shift_turn(i, t):
                if t == 1:
                    wait(pe, shift_t_done, NT * i + 1)
                elif has(i + 1):
                    wait(pe, q_lo, DC * (i + 1) + 2)
                else:
                    wait(pe, shift_t_done, NT * i)
                wait(pe, shift_ready, NT * i + t + 1)
                pe.transpose(proj[0][0:NH, 0:P], shift[:, t, :], ident[:, :]).then_inc(shift_t_ready, 1)

            def out_project(m, t):
                if t == 1:
                    wait(pe, o_done, NT * m + 1)
                elif has(m + 2):
                    wait(pe, q_lo, DC * (m + 2) + 4)
                else:
                    wait(pe, o_done, NT * m)
                wait(pe, ht_lo, NT * m + t + 1)
                for c in range(DC):
                    mm = three(proj[1][:, :], [h[:, t, c, :] for h in ht], [h[:, c, :] for h in wo], c == 0, c == DC - 1)
                mm.then_inc(o_ready, 1)

            def first_in_proj0(n):
                if has(n - 2):
                    wait(pe, shift_t_done, NT * (n - 1))
                elif has(n - 1):
                    wait(pe, q_lo, DC * (n - 1) + 2)

            def first_in_proj1(n):
                if has(n - 3):
                    wait(pe, o_done, NT * (n - 2))
                elif has(n - 1):
                    wait(pe, q_lo, DC * n)

            def turn(n, t):
                if cross:
                    wait(pe, (k_lo, v_done)[t], n + 1)
                else:
                    (first_in_proj0, first_in_proj1)[t](n)
                wait(pe, xn_ready, NT * n + t + 1)
                for c in range(DC):
                    mm = pe.transpose(proj[t][:, c * P:(c + 1) * P], x_tile[:, t, c * P:(c + 1) * P], ident[:, :])
                mm.then_inc(t_ready, 1)

            def q_project(n, half):
                wait(pe, xt_lo, NT * (n + 1))
                if not cross:
                    wait(pe, (k_lo, v_done)[half], n + 1)
                for c in (2 * half, 2 * half + 1):
                    for k in range(DC):
                        mm = three(proj[half][:, (c % 2) * S:(c % 2 + 1) * S], [h[:, k, c * P:(c + 1) * P] for h in wq],
                                   [h[:, k, :] for h in xt], k == 0, k == DC - 1)
                mm.then_inc(q_ready, 1)

            def k_project(n):
                if cross:
                    first_in_proj0(n)
                    wait(pe, src_lo, n + 1)
                else:
                    wait(pe, xt_lo, NT * (n + 1))
                for k in range(DC):
                    mm = three(proj[0][:, 0:S], [h[:, k, 0:P] for h in wkv], [h[:, k, :] for h in xt], k == 0, k == DC - 1)
                mm.then_inc(k_ready, 1)

            def v_project(n):
                if cross:
                    first_in_proj1(n)
                for t in range(NT):
                    for k in range(DC):
                        mm = three(proj[1][:, t * VD:(t + 1) * VD], [h[:, k, t * P:(t + 1) * P] for h in xt],
                                   [h[:, k, P:P + VD] for h in wkv], k == 0, k == DC - 1)
                mm.then_inc(v_ready, 1)

            def step(i, par):
                n, b = i + 1, i - 1
                jobs = {
                    "t0": (n, lambda: turn(n, 0)), "t1": (n, lambda: turn(n, 1)), "k": (n, lambda: k_project(n)), "v": (n, lambda: v_project(n)),
                    "q0": (n, lambda: q_project(n, 0)), "q1": (n, lambda: q_project(n, 1)),
                    "shift0": (i, lambda: shift_turn(i, 0)), "shift1": (i - 1, lambda: shift_turn(i - 1, 1)),
                    "out0": (i - 1, lambda: out_project(i - 1, 0)), "out1": (i - 2, lambda: out_project(i - 2, 1)),
                }
                for u in range(NU):
                    if has(b):
                        score_unit(b, 1 - par, u)
                    if has(i):
                        max_unit(i, par, u)
                    if u == 1 and has(i - 2):
                        pv_group(i - 2, par, NG - 1)
                    if u % 4 == 1 and u > 4 and has(b):
                        pv_group(b, 1 - par, u // 4 - 1)
                    for job in A.pe_plan.get(u, ()):
                        m, do = jobs[job]
                        if has(m):
                            do()

            steps(pe, step)


def build_ffn(nc, B, x_in, x_out, w0, b0, w1, b1):
    F = w0.shape[1]
    FC = F // P
    TOK = 512
    TT = TOK // P
    N = B * S // TOK
    RING = 4
    LAG = 2
    with ExitStack() as es:
        def sb(name, shape, dt):
            return es.enter_context(nc.sbuf_tensor(f"ffn_{name}", shape, dt))

        def pb(name, shape, dt=F32):
            return es.enter_context(nc.psum_tensor(f"ffn_{name}", shape, dt))

        def sem(name):
            return es.enter_context(nc.semaphore(f"ffn_{name}"))

        stage = sb("stage", [P, 2, F], F32)
        w0s = [sb(f"w0{n}", [P, DC, F], F32R) for n in range(2)]
        w1s = [sb(f"w1{n}", [P, FC, D], F32R) for n in range(2)]
        bias0 = sb("bias0", [P, FC], F32)
        bias1 = sb("bias1", [P, D], F32)
        ident = sb("ident", [P, P], F32)
        ident16 = sb("ident16", [P, P], F16)
        x_tile = sb("x_tile", [P, TT, D], F32)
        stats = sb("stats", [P, TT, 6], F32)
        mv = sb("mv", [P, TT, 2], F32)
        veps = sb("veps", [P, TT], F32)
        root = sb("root", [P, TT], F32)
        r0 = sb("r0", [P, TT], F32)
        r1 = sb("r1", [P, TT], F32)
        r2 = sb("r2", [P, TT], F32)
        gate = sb("gate", [P, 1], F32)
        rstd = sb("rstd", [P, TT], F32)
        xn = sb("xn", [P, TT, D], F16)
        xt = sb("xt", [P, DC, TOK], F32R)
        h16 = sb("h16", [P, 2, TOK], F16)
        hid = sb("hid", [P, RING, TOK], F32R)
        e16 = sb("e16", [P, TT, D], F16)

        turn_ps = pb("turn_ps", [P, 2, 2 * D], F16)
        up_ps = [pb(f"up{n}", [P, TOK]) for n in range(2)]
        down_ps = [pb(f"down{n}", [P, D]) for n in range(TT)]

        biases_in, w_in, w_hi, w_lo = sem("biases_in"), [sem("w_in0"), sem("w_in1")], sem("w_hi"), sem("w_lo")
        ident_set, ident16_set, rstd_ready = sem("ident_set"), sem("ident16_set"), sem("rstd_ready")
        x_loaded, ln_step, var_ready, root_done, xn_ready = sem("x_loaded"), sem("ln_step"), sem("var_ready"), sem("root_done"), sem("xn_ready")
        t_ready, xt_ready = sem("t_ready"), sem("xt_ready")
        up_ready, gelu_done, hid_ready, used = sem("up_ready"), sem("gelu_done"), sem("hid_ready"), sem("used")
        down_ready, e_ready, out_ready, stored = sem("down_ready"), sem("e_ready"), sem("out_ready"), sem("stored")
        block = es.enter_context(nc.Block())
        x_rows = x_in.rearrange("b s d -> (b s) d").rearrange("(n t p) d -> n p t d", t=TT, p=P)
        o_rows = x_out.rearrange("b s d -> (b s) d").rearrange("(n t p) d -> n p t d", t=TT, p=P)
        pieces = ([(w0s, c, w0[c * P:(c + 1) * P, :]) for c in range(DC)]
                  + [(w1s, g, w1[g * 4 * P:(g + 1) * 4 * P, :]) for g in range(FC // 4)])

        def part_of(w, k, hi):
            return w[hi][:, k, :] if w is w0s else w[hi][:, 4 * k:4 * k + 4, :].rearrange("p g n -> p (g n)")

        def steps(engine, step):
            step(0)
            with engine.Fori(1, N) as i:
                step(i)

        @block.sync
        def _(sp):
            sp.dma_start(x_tile[:, :, :], x_rows[0]).then_inc(x_loaded, 16)
            for n, (w, k, src) in enumerate(pieces):
                wait(sp, w_lo, n - 1)
                dst = stage[:, n % 2, :] if w is w0s else stage[:, n % 2, :].rearrange("p (g n) -> p g n", g=4)
                sp.dma_start(dst, src if w is w0s else src.rearrange("(g p) n -> p g n", p=P)).then_inc(w_in[n % 2], 16)
            sp.dma_start(bias0[:, :], b0).then_inc(biases_in, 16)
            sp.dma_start(bias1[:, :], b1.partition_broadcast(P)).then_inc(biases_in, 16)

            def step(i):
                if not isinstance(i, int):
                    sp.wait_ge(stored, 16 * i)
                    sp.dma_start(x_tile[:, :, :], x_rows[bass.ds(i, 1), :, :, :].rearrange("a p t d -> (a p) t d")).then_inc(x_loaded, 16)
                wait(sp, out_ready, TT * (i + 1))
                dst = o_rows[0] if isinstance(i, int) else o_rows[bass.ds(i, 1), :, :, :].rearrange("a p t d -> (a p) t d")
                sp.dma_start(dst, x_tile[:, :, :]).then_inc(stored, 16)

            steps(sp, step)
            sp.wait_ge(stored, 16 * N)

        @block.gpsimd
        def _(pool):
            pool.memset(ident[:, :], 0.0).then_inc(ident_set, 1)
            pool.wait_ge(ident_set, 1)
            pool.affine_select(out=ident[:, :], in_=ident[:, :], compare_op=ALU.not_equal, fill=1.0, base=0,
                               pattern=[[-1, P]], channel_multiplier=1).then_inc(ident_set, 1)

            def step(i):
                for t in range(TT):
                    wait(pool, e_ready, TT * i + t + 1)
                    pool.tensor_tensor(x_tile[:, t, :], x_tile[:, t, :], e16[:, t, :], ALU.add).then_inc(out_ready, 1)

            steps(pool, step)

        @block.scalar
        def _(act):
            for n, (w, k, _) in enumerate(pieces):
                act.wait_ge(w_in[n % 2], 16 * (n // 2 + 1))
                act.activation(part_of(w, k, 0), stage[:, n % 2, :], ACT.Copy).then_inc(w_hi, 1)
            act.wait_ge(biases_in, 32)

            def step(i):
                wait(act, var_ready, i + 1)
                act.activation(root[:, :], veps[:, :], ACT.Sqrt).then_inc(root_done, 1)
                for t in range(TT):
                    wait(act, t_ready, TT * i + t + 1)
                    act.activation(xt[:, :, t * P:(t + 1) * P], turn_ps[:, t % 2, 0:D].rearrange("p (c q) -> p c q", c=DC), ACT.Copy).then_inc(xt_ready, 1)
                for f in range(FC):
                    wait(act, up_ready, FC * i + f + 1)
                    wait(act, hid_ready, FC * i + f - 1)
                    act.activation(h16[:, f % 2, :], up_ps[f % 2][:, :], ACT.Gelu, bias=bias0[:, f:f + 1]).then_inc(gelu_done, 1)

            steps(act, step)

        @block.vector
        def _(dve):
            for n, (w, k, _) in enumerate(pieces):
                dve.wait_ge(w_hi, n + 1)
                dve.tensor_tensor(part_of(w, k, 1), stage[:, n % 2, :], part_of(w, k, 0).bitcast(F32), ALU.subtract).then_inc(w_lo, 1)
            dve.wait_ge(ident_set, 2)
            dve.tensor_copy(ident16[:, :], ident[:, :]).then_inc(ident16_set, 1)
            dve.wait_ge(biases_in, 32)

            def step(i):
                wait(dve, x_loaded, 16 * (i + 1))
                for t in range(TT):
                    dve.bn_stats(stats[:, t, :], x_tile[:, t, :]).then_inc(ln_step, 1)
                base = i * (2 * TT + 4)
                wait(dve, ln_step, base + TT)
                dve.memset(gate[:, :], 0.0)
                for t in range(TT):
                    dve.bn_aggr(mv[:, t, :], stats[:, t, :]).then_inc(ln_step, 1)
                base = base + 2 * TT
                wait(dve, ln_step, base)
                dve.tensor_scalar(veps[:, :], mv[:, :, 1], EPS, None, ALU.add).then_inc(var_ready, 1)
                wait(dve, root_done, i + 1)
                dve.reciprocal(r0[:, :], root[:, :]).then_inc(ln_step, 1)
                wait(dve, ln_step, base + 1)
                dve.tensor_tensor(r1[:, :], r0[:, :], r0[:, :], ALU.mult).then_inc(ln_step, 1)
                wait(dve, ln_step, base + 2)
                dve.tensor_tensor(r2[:, :], r1[:, :], veps[:, :], ALU.mult).then_inc(ln_step, 1)
                wait(dve, ln_step, base + 3)
                dve.tensor_scalar(r1[:, :], r2[:, :], -0.5, 1.5, ALU.mult, ALU.add).then_inc(ln_step, 1)
                wait(dve, ln_step, base + 4)
                dve.tensor_tensor(rstd[:, :], r1[:, :], r0[:, :], ALU.mult).then_inc(rstd_ready, 1)
                wait(dve, rstd_ready, i + 1)
                wait(dve, t_ready, TT * i)
                for t in range(TT):
                    dve.tensor_scalar(xn[:, t, :], x_tile[:, t, :], mv[:, t, 0:1], rstd[:, t:t + 1], ALU.subtract, ALU.mult).then_inc(xn_ready, 1)
                for f in range(FC):
                    wait(dve, gelu_done, FC * i + f + 1)
                    wait(dve, used, FC * i + f - RING + 1)
                    dve.tensor_copy(hid[:, f % RING, :], h16[:, f % 2, :]).then_inc(hid_ready, 1)
                wait(dve, out_ready, TT * i)
                for t in range(TT):
                    wait(dve, down_ready, i + 1)
                    dve.tensor_tensor(e16[:, t, :], down_ps[t][:, :], bias1[:, :], ALU.add).then_inc(e_ready, 1)

            steps(dve, step)

        @block.tensor
        def _(pe):
            pe.wait_ge(ident16_set, 1)
            pe.wait_ge(w_lo, len(pieces))

            def step(i):
                for t in range(TT):
                    wait(pe, xn_ready, TT * i + t + 1)
                    wait(pe, xt_ready, TT * i + t - 1)
                    for c in range(DC):
                        mm = pe.transpose(turn_ps[:, t % 2, c * P:(c + 1) * P], xn[:, t, c * P:(c + 1) * P], ident16[:, :])
                    mm.then_inc(t_ready, 1)
                wait(pe, xt_ready, TT * (i + 1))
                for f in range(FC + LAG):
                    if f < FC:
                        wait(pe, gelu_done, FC * i + f - 1)
                        for k in range(DC):
                            for h in range(2):
                                mm = pe.matmul(up_ps[f % 2][:, :], w0s[h][:, k, f * P:(f + 1) * P], xt[:, k, :],
                                               start=(k == 0 and h == 0), stop=(k == DC - 1 and h == 1))
                        mm.then_inc(up_ready, 1)
                    g = f - LAG
                    if g >= 0:
                        wait(pe, hid_ready, FC * i + g + 1)
                        if g == 0:
                            wait(pe, e_ready, TT * i)
                        for t in range(TT):
                            for h in range(2):
                                mm = pe.matmul(down_ps[t][:, :], hid[:, g % RING, t * P:(t + 1) * P], w1s[h][:, g, :],
                                               start=(g == 0 and h == 0), stop=(g == FC - 1 and h == 1))
                        mm.then_inc(used, 1)
                wait(pe, used, FC * (i + 1))
                pe.nop().then_inc(down_ready, 1)

            steps(pe, step)


def build(nc, a, out):
    B = a["x"].shape[0]
    x1 = nc.dram_tensor("x_after_self", a["x"].shape, F32, kind="Internal").ap()
    x2 = nc.dram_tensor("x_after_cross", a["x"].shape, F32, kind="Internal").ap()
    build_attention(nc, Attention("self", 32, True), B, a["x"], x1,
                    dict(q=a["self_wq"], kv=a["self_wkv"], o=a["self_wo"], bq=a["self_bq"], bk=a["self_bk"], bv=a["self_bv"], bo=a["self_bo"]))
    build_attention(nc, Attention("cross", 16, False), B, x1, x2,
                    dict(q=a["cross_wq"], kv=a["cross_wkv"], o=a["cross_wo"], bq=a["cross_bq"], bk=a["cross_bk"], bv=a["cross_bv"], bo=a["cross_bo"]),
                    ctx_t=a["ctx_t"], mask=a["mask"], mask_t=a["mask_t"], pad=a["pad"], pad_col=a["pad_col"])
    build_ffn(nc, B, x2, out, a["w0"], a["b0"], a["w1"], a["b1"])


def kernel(**inputs):
    import numpy as np
    import concourse.bacc as bacc
    from concourse.bass_utils import run_bass_kernel_spmd

    i = {k: np.asarray(v) for k, v in inputs.items()}
    order = np.arange(512).reshape(8, 4, 16).transpose(1, 0, 2).reshape(512)
    wqkv, bqkv = i["L0_attn_Wqkv_w"], i["L0_attn_Wqkv_b"]
    lay = {
        "x": i["x"],
        "self_wq": wqkv[:512].T, "self_wkv": np.concatenate([np.tile(wqkv[512:544].T, (1, 4)), wqkv[544:].T], 1),
        "self_wo": i["L0_attn_out_w"].T,
        "self_bq": bqkv[:512].reshape(4, 128).T, "self_bk": np.tile(bqkv[512:544], 4).reshape(128, 1),
        "self_bv": bqkv[544:], "self_bo": i["L0_attn_out_b"],
        "cross_wq": i["L0_xattn_Wq"].T[:, order], "cross_wkv": np.concatenate([i["L0_xattn_Wk"].T, i["L0_xattn_Wv"].T], 1),
        "cross_wo": i["L0_xattn_Wo"].T[order],
        "cross_bq": i["L0_xattn_bq"][order].reshape(4, 128).T, "cross_bk": i["L0_xattn_bk"].reshape(128, 1),
        "cross_bv": i["L0_xattn_bv"], "cross_bo": i["L0_xattn_bo"],
        "ctx_t": i["ctx_2048"].transpose(0, 2, 1),
        "mask": i["mask_SxS2_bc0"].view(np.uint32), "mask_t": np.ascontiguousarray(i["mask_SxS2_bc0"].T).view(np.uint32),
        "pad": i["mask_BxS2_bk0"].view(np.uint32),
        "pad_col": np.ascontiguousarray(i["mask_BxS2_bk0"].reshape(32, 128).T).view(np.uint32),
        "w0": i["L0_ffn_W0"].T, "b0": i["L0_ffn_bias0"].reshape(16, 128).T,
        "w1": i["L0_ffn_W1"].T, "b1": i["L0_ffn_bias1"],
    }
    nc = bacc.Bacc("TRN2", target_bir_lowering=False, num_devices=1)
    arrays, aps = {}, {}
    for name, v in lay.items():
        v = np.ascontiguousarray(v)
        arrays[f"in_{name}"] = v
        aps[name] = nc.dram_tensor(f"in_{name}", v.shape, mybir.dt.from_np(v.dtype), kind="ExternalInput").ap()
    out = nc.dram_tensor("out_x", i["x"].shape, F32, kind="ExternalOutput").ap()
    build(nc, aps, out)
    r = run_bass_kernel_spmd(nc, [arrays], core_ids=[0])
    return r.results[0]["out_x"]
```

```python
from contextlib import ExitStack

import concourse.bass as bass
from concourse import mybir

ALU = mybir.AluOpType
ACT = mybir.ActivationFunctionType
AX = mybir.AxisListType
F32 = mybir.dt.float32
F32R = mybir.dt.float32r
BF16 = mybir.dt.bfloat16
F16 = mybir.dt.float16
U32 = mybir.dt.uint32
U8 = mybir.dt.uint8
I32 = mybir.dt.int32

P = 128
D = 512
DC = D // P
S = 256
NT = S // P
BIG = 1e30
SHIFT_MAX = 1e29
FLOOR = 3e38
EPS = 1e-5
STACK = 97


class Attention:

    def __init__(self, name, head_dim, causal):
        self.name = name
        self.HD = head_dim
        self.NB = P // head_dim
        self.NH = self.NB * DC
        self.causal = causal
        self.KB = 1 if causal else self.NB
        self.VD = head_dim * self.KB
        self.scale = float(head_dim) ** -0.5
        self.shift_row = 3 * head_dim
        self.max_units = []
        for qt in range(NT):
            width = P * (qt + 1) if causal else S
            n = 512 // width
            self.max_units += [(qt, c, b, n, width) for c in range(DC) for b in range(0, self.NB, n)]
        self.groups = []
        halves = self.NB // 4
        for qt in range(NT):
            key_tiles = range(qt + 1) if causal else range(NT)
            for half in range(halves):
                blocks = [halves * j + half for j in range(4)]
                for kt in key_tiles:
                    first, last = (half, kt) == (0, 0), (half, kt) == (halves - 1, key_tiles[-1])
                    self.groups.append((qt, half, blocks, kt, first, last))
        self.NG = len(self.groups)
        self.NU = 4 * self.NG
        assert self.NU == len(self.max_units)
        self.groups_of_tile0 = sum(g[0] == 0 for g in self.groups)
        self.max_units_of_tile0 = sum(u[0] == 0 for u in self.max_units)
        if causal:
            self.sp_plan = ["x", "q1", "shift1", "store1", "qout", "res0", "res1", "k", "q0", "shift0", "store0"]
            self.pe_plan = {0: ["shift1"], 3: ["out1", "t0", "t1"], 6: ["k"], 7: ["v", "q0"], 8: ["q1", "shift0"], 11: ["out0"]}
            self.act_plan = {0: ["shift1", "head1"], 4: ["t0"], 5: ["t1"], 6: ["k", "q0"], 7: ["head0"], 9: ["shift0", "q1"]}
            self.dve_plan = {1: ["inv10", "inv11", "norm1", "stats", "head1", "root", "apply"], 2: ["out1"], 3: ["t0"], 4: ["v_use", "t1"], 5:
                             ["inv00", "k", "inv01"], 6: ["norm0"], 7: ["v", "q0"], 9: ["q1", "head0"], 10: ["kb0"], 11: ["kb1", "out0"]}
        else:
            self.sp_plan = ["x", "src", "kout", "q1", "k", "qout", "pad", "res0", "shift1", "store1", "res1", "q0", "shift0", "store0"]
            self.pe_plan = {4: ["shift1"], 6: ["k"], 9: ["out1"], 10: ["v"], 13: ["t0"], 16: ["t1"], 19: ["q0"], 21: ["q1"], 25: ["shift0"],
                            28: ["out0"]}
            self.act_plan = {0: ["mix1"], 2: ["src", "shift1"], 5: ["k"], 8: ["head1"], 15: ["t0"], 17: ["t1"], 18: ["mix0"], 20: ["q0"], 21:
                             ["q1"], 25: ["head0"], 26: ["shift0"]}
            self.dve_plan = {2: ["mix1"], 3: ["inv10"], 4: ["src"], 5: ["inv11"], 6: ["norm1"], 7: ["v_use", "head1"], 8: ["mask"], 9:
                             ["out1"], 10: ["stats", "root"], 11: ["k", "apply"], 14: ["v"], 16: ["t0"], 17: ["t1", "kb0"], 19: ["mix0", "inv00"], 21:
                             ["inv01"], 22: ["q0"], 24: ["norm0"], 25: ["q1", "head0"], 28: ["kb1"], 29: ["out0"]}


def wait(engine, sem, value):
    if isinstance(value, int) and value <= 0:
        return
    engine.wait_ge(sem, value)


def spread(ap, times):
    return ap.unsqueeze(1).broadcast_to([ap.shape[0], times, ap.shape[1]])


def inverse_root(dve, var, tiles, sem, base):
    r, a, h = tiles
    dve.tensor_scalar(h, var, EPS, None, ALU.add).then_inc(sem, 1)
    wait(dve, sem, base + 1)
    dve.tensor_scalar(a.bitcast(I32), h.bitcast(I32), 1, None, ALU.arith_shift_right).then_inc(sem, 1)
    wait(dve, sem, base + 2)
    dve.tensor_scalar(r.bitcast(I32), a.bitcast(I32), -1, 0x5F3759DF, ALU.mult, ALU.add)
    dve.tensor_scalar(h, h, -0.5, None, ALU.mult).then_inc(sem, 1)
    for k in range(3):
        wait(dve, sem, base + 3 + 3 * k)
        dve.tensor_tensor(a, r, r, ALU.mult).then_inc(sem, 1)
        wait(dve, sem, base + 4 + 3 * k)
        dve.tensor_tensor(a, a, h, ALU.mult).then_inc(sem, 1)
        wait(dve, sem, base + 5 + 3 * k)
        dve.scalar_tensor_tensor(out=r, in0=a, scalar=1.5, in1=r, op0=ALU.add, op1=ALU.mult).then_inc(sem, 1)


def build_attention(nc, A, B, x_in, x_out, w, ctx_t=None, mask=None, mask_t=None, pad=None, pad_col=None):
    HD, NB, KB, VD, NH, NG, NU = A.HD, A.NB, A.KB, A.VD, A.NH, A.NG, A.NU
    cross = not A.causal
    with ExitStack() as es:
        def sb(name, shape, dt):
            return es.enter_context(nc.sbuf_tensor(f"{A.name}_{name}", shape, dt))

        def pb(name, shape, dt=F32):
            return es.enter_context(nc.psum_tensor(f"{A.name}_{name}", shape, dt))

        def sem(name):
            return es.enter_context(nc.semaphore(f"{A.name}_{name}"))

        wq = [sb(f"wq{n}", [P, DC, D], F32R) for n in range(2)]
        wkv = [sb(f"wkv{n}", [P, DC, P + VD], F32R) for n in range(2)]
        wo = [sb(f"wo{n}", [P, DC, D], F32R) for n in range(2)]
        bq = sb("bq", [P, DC], F32)
        bk = sb("bk", [P, 1], F32)
        bv = sb("bv", [P, VD], F32)
        bo = sb("bo", [P, D], F32)
        ident = sb("ident", [P, P], F32)
        ident16 = sb("ident16", [P, P], BF16)
        block_mask = sb("block_mask", [P, NB], F32)
        if A.causal:
            ones_v = sb("ones_v", [P, 2, 32], F32)
        else:
            lane_half = sb("lane_half", [P, 2], F32)
        ones_row = sb("ones_row", [1, S], F32R)
        mask_q0 = sb("mask_q0", [P, NT, S], BF16)
        mask_k0 = sb("mask_k0", [P, NT, S], BF16)
        x_tile = sb("x_tile", [P, NT, D], F32)
        stats = sb("stats", [P, NT, 6], F32)
        mv = sb("mv", [P, NT, 2], F32)
        square = sb("square", [P, NT], F32)
        half_var = sb("half_var", [P, NT], F32)
        gate = sb("gate", [P, 6], F32)
        rstd = sb("rstd", [P, NT], F32)
        xt = [sb(f"xt{n}", [P, DC, S], F32R) for n in range(2)]
        q_parts = [[sb(f"q{m}{n}", [P, DC, S], F32R) for n in range(2)] for m in range(2)]
        k_parts = [sb(f"k{n}", [P, S], F32R) for n in range(2)]
        k_blocks = [sb(f"k_blocks{m}", [P, NB, S], F32R) for m in range(2)]
        v_new = sb("v_new", [P, NT, VD], F32)
        v_use = [sb(f"v_use{m}", [P, NT, KB, 32], F32) for m in range(2)]
        row_max = sb("row_max", [P, NT, NB, DC], F32)
        shift = sb("shift", [P, NT, NH], F32)
        shift_t = sb("shift_t", [NH, NT, P], F32R)
        q_stack = sb("q_stack", [STACK, NT, NB * DC, P], F32R)
        k_stack = [sb(f"k_stack{m}", [STACK, KB, S], F32R) for m in range(2)]
        probs = sb("probs", [P, 2, 4, 512], F32)
        recip = sb("recip", [P, 512], F32)
        heads = sb("heads", [P, NT, 512], F32)
        ht = [sb(f"ht{n}", [P, NT, DC, P], F32R) for n in range(2)]
        x_res = sb("x_res", [P, NT, D], F32)
        if cross:
            src = sb("src", [P, DC, S], F32)
            mask_words = sb("mask_words", [P, 2, NT, S // 4], U32)
            pad_words = sb("pad_words", [P, S // 4], U32)
            pad_f = sb("pad_f", [P, S], F32)
            padc_words = sb("padc_words", [P, B * NT // 4], U32)
            padc_f = sb("padc_f", [P, B * NT], F32)
            mask_q = [sb(f"mask_q_of{m}", [P, NT, S], BF16) for m in range(2)]
            mask_k = [sb(f"mask_k_of{m}", [P, NT, S], BF16) for m in range(2)]
        else:
            mask_q, mask_k = [mask_q0] * 2, [mask_k0] * 2
        staged = probs[:, :, :, :].rearrange("p a b n -> p (a b n)")
        stages = [(wq, D, staged[:, 0:DC * D]), (wkv, P + VD, staged[:, DC * D:DC * (D + P + VD)]), (wo, D, staged[:, 0:DC * D])]
        stages = [(part, st.rearrange("p (c n) -> p c n", c=DC)) for part, _, st in stages]

        proj = [pb(f"proj{n}", [P, 512]) for n in range(2)]
        max_ps = [pb(f"max{n}", [P, 512]) for n in range(2)]
        score_ps = [pb(f"score{n}", [P, 512]) for n in range(2)]
        heads_ps = pb("heads_ps", [P, 512])
        sums_ps = pb("sums_ps", [P, 512])
        even_ps, odd_ps = heads_ps, sums_ps
        Q_ROWS_IN, K_ROWS_IN = 16 * 2 * NT, 16 * 2
        q_rows = nc.dram_tensor(f"{A.name}_q_rows", [2, 2, NT, P, DC, P], F32, kind="Internal").ap()
        k_rows = nc.dram_tensor(f"{A.name}_k_rows", [2, 2, P, S], F32, kind="Internal").ap()
        shift_rows = nc.dram_tensor(f"{A.name}_shift_rows", [NT, NH, P], F32, kind="Internal").ap()

        biases_in, masks_in, ones_in = sem("biases_in"), sem("masks_in"), sem("ones_in")
        w_in, w_hi, w_lo = [sem(f"w_in{n}") for n in range(3)], sem("w_hi"), sem("w_lo")
        ident_set, masks_set, consts_set, stacks_set = sem("ident_set"), sem("masks_set"), sem("consts_set"), sem("stacks_set")
        x_loaded, src_loaded, pad_loaded = sem("x_loaded"), sem("src_loaded"), sem("pad_loaded")
        ln_step, xn_ready = sem("ln_step"), sem("xn_ready")
        t_ready, xt_hi, xt_lo = sem("t_ready"), sem("xt_hi"), sem("xt_lo")
        src_hi, src_lo = sem("src_hi"), sem("src_lo")
        q_ready, q_hi, q_lo = sem("q_ready"), sem("q_hi"), sem("q_lo")
        k_ready, k_hi, k_lo, kb_ready = sem("k_ready"), sem("k_hi"), sem("k_lo"), sem("kb_ready")
        v_ready, v_done = sem("v_ready"), sem("v_done")
        padf_set, mask_q_ready, mask_k_ready = sem("padf_set"), sem("mask_q_ready"), sem("mask_k_ready")
        max_ready, max_done, shift_ready, shift_t_ready, shift_t_done = (
            sem("max_ready"), sem("max_done"), sem("shift_ready"), sem("shift_t_ready"), sem("shift_t_done"))
        q_spilled, k_spilled = sem("q_spilled"), sem("k_spilled")
        k_stacked, v_use_ready = sem("k_stacked"), sem("v_use_ready")
        q_stacked, shift_spilled, shift_stacked = ([sem(f"{n}{t}") for t in range(NT)] for n in ("q_stacked", "shift_spilled", "shift_stacked"))
        score_ready, exp_done, pv_done = sem("score_ready"), sem("exp_done"), sem("pv_done")
        odd_copied, mixed, swapped = sem("odd_copied"), sem("mixed"), sem("swapped")
        recip_done, heads_ready, ht_hi, ht_lo = sem("recip_done"), sem("heads_ready"), sem("ht_hi"), sem("ht_lo")
        res_biased, o_ready, o_done = sem("res_biased"), sem("o_ready"), sem("o_done")
        res_loaded, stored = ([sem(f"{n}{t}") for t in range(NT)] for n in ("res_loaded", "stored"))
        block = es.enter_context(nc.Block())

        def rows(dram, i, t):
            return dram[bass.ds(i, 1), t * P:(t + 1) * P, :].rearrange("a p d -> (a p) d")

        def has(m):
            return not isinstance(m, int) or 0 <= m < B

        def steps(engine, step):
            for i in (-1, 0, 1, 2):
                step(i, i % 2)
            with engine.Fori(3, B - 2, 2) as i:
                step(i, 1)
                step(i + 1, 0)
            for i in (B - 1, B, B + 1):
                step(i, i % 2)

        @block.sync
        def _(sp):
            def load_weights(n, dram):
                sp.dma_start(stages[n][1], dram.rearrange("(c p) n -> p c n", p=P)).then_inc(w_in[n], 16)

            load_weights(0, w["q"])
            load_weights(1, w["kv"])
            sp.dma_start(bq[:, :], w["bq"]).then_inc(biases_in, 16)
            sp.dma_start(bk[:, :], w["bk"]).then_inc(biases_in, 16)
            sp.dma_start(bv[:, :], w["bv"].partition_broadcast(P)).then_inc(biases_in, 16)
            sp.dma_start(bo[:, :], w["bo"].partition_broadcast(P)).then_inc(biases_in, 16)
            if cross:
                sp.dma_start(mask_words[:, 0], mask.rearrange("(t p) k -> p t k", p=P)).then_inc(masks_in, 16)
                sp.dma_start(mask_words[:, 1], mask_t.rearrange("(t p) q -> p t q", p=P)).then_inc(masks_in, 16)
                sp.dma_start(padc_words[:, :], pad_col).then_inc(masks_in, 16)

            def spill_q(m, par):
                wait(sp, q_lo, DC * (m + 1))
                for t in range(NT):
                    wait(sp, q_stacked[t], 16 * 3 * m - 16 * 3)
                for part in range(2):
                    for t in range(NT):
                        sp.dma_start(q_rows[par, part, t], q_parts[par][part][:, :, t * P:(t + 1) * P].bitcast(F32)).then_inc(q_spilled, 16)

            def spill_k(m, par):
                wait(sp, k_lo, m + 1)
                wait(sp, k_stacked, 16 * 3 * m - 16 * 3)
                for part in range(2):
                    sp.dma_start(k_rows[par, part], k_parts[part][:, :].bitcast(F32)).then_inc(k_spilled, 16)

            def stack_q(m, par, t):
                for part, at in ((0, 0), (1, 1), (0, 2)):
                    sp.dma_start(q_stack[at * HD:(at + 1) * HD, t, 0:NH, :].rearrange("d (g c) q -> d g (c q)", c=DC).bitcast(F32),
                                 q_rows[par, part, t].rearrange("(g d) c q -> d g (c q)", d=HD)).then_inc(q_stacked[t], 16)

            def stack_shift(m, t):
                wait(sp, shift_t_done, NT * m + t + 1)
                sp.dma_start(shift_rows[t], shift_t[:, t, :].bitcast(F32)).then_inc(shift_spilled[t], 16)
                wait(sp, shift_spilled[t], 16 * (m + 1))
                sp.dma_start(q_stack[A.shift_row:A.shift_row + 1, t, 0:NH, :].bitcast(F32), shift_rows[t:t + 1]).then_inc(shift_stacked[t], 16)

            def set_up_rest():
                sp.wait_ge(w_lo, 1)
                load_weights(2, w["o"])
                sp.wait_ge(stacks_set, 5)
                for m in range(2):
                    for g in range(KB):
                        sp.dma_start(k_stack[m][A.shift_row:A.shift_row + 1, g, :].bitcast(F32), ones_row[0:1, :].bitcast(F32)).then_inc(ones_in, 16)

            def load_x(n):
                wait(sp, t_ready, NT * n)
                for t in range(NT):
                    sp.dma_start(x_tile[:, t, :], rows(x_in, n, t)).then_inc(x_loaded, 16)

            def load_src(n):
                wait(sp, src_lo, n)
                sp.dma_start(src[:, :, :], ctx_t[bass.ds(n, 1), :, :].rearrange("a (c p) s -> p (a c) s", p=P)).then_inc(src_loaded, 16)

            def load_pad(n):
                wait(sp, padf_set, n)
                sp.dma_start(pad_words[:, :], pad[bass.ds(n, 1), :].rearrange("a s -> (a s)").partition_broadcast(P)).then_inc(pad_loaded, 16)

            def stack_q1(m, par):
                wait(sp, score_ready, NU * m)
                stack_q(m, par, 1)

            def stack_q0(m, par, has_before):
                if has_before:
                    wait(sp, score_ready, NU * m + (4 * A.groups_of_tile0 - NU))
                wait(sp, q_spilled, (m + 3) * Q_ROWS_IN - 2 * Q_ROWS_IN)
                stack_q(m, par, 0)

            def stack_k(m, par, has_before):
                if not cross:
                    wait(sp, k_lo, m + 1)
                if has_before:
                    wait(sp, score_ready, NU * (m - 1))
                else:
                    wait(sp, ones_in, 32 * KB)
                if cross:
                    wait(sp, k_spilled, (m + 2) * K_ROWS_IN - K_ROWS_IN)
                for part, at in ((0, 0), (0, 1), (1, 2)):
                    of = k_rows[par, part].rearrange("(g d) s -> d g s", d=HD) if cross else k_parts[part][0:HD, :].unsqueeze(1).bitcast(F32)
                    sp.dma_start(k_stack[par][at * HD:(at + 1) * HD, :, :].bitcast(F32), of).then_inc(k_stacked, 16)

            def load_res(m, t):
                wait(sp, stored[t], 16 * m)
                sp.dma_start(x_res[:, t, :], rows(x_in, m, t)).then_inc(res_loaded[t], 16)

            def store(m, t):
                wait(sp, o_done, NT * m + t + 1)
                sp.dma_start(rows(x_out, m, t), x_res[:, t, :]).then_inc(stored[t], 16)

            def step(i, par):
                n = i + 1
                if isinstance(i, int) and i == 0:
                    set_up_rest()
                jobs = {
                    "x": (n, lambda: load_x(n)), "src": (n, lambda: load_src(n)), "pad": (n, lambda: load_pad(n)),
                    "kout": (i, lambda: spill_k(i, par)), "qout": (i, lambda: spill_q(i, par)),
                    "q1": (i - 1, lambda: stack_q1(i - 1, 1 - par)), "k": (i, lambda: stack_k(i, par, has(i - 1))),
                    "shift1": (i - 1, lambda: stack_shift(i - 1, 1)), "res0": (i - 1, lambda: load_res(i - 1, 0)),
                    "store1": (i - 2, lambda: store(i - 2, 1)), "res1": (i - 1, lambda: load_res(i - 1, 1)),
                    "q0": (i, lambda: stack_q0(i, par, has(i - 1))), "shift0": (i, lambda: stack_shift(i, 0)),
                    "store0": (i - 1, lambda: store(i - 1, 0)),
                }
                for job in A.sp_plan:
                    m, do = jobs[job]
                    if has(m):
                        do()

            steps(sp, step)
            for t in range(NT):
                sp.wait_ge(stored[t], 16 * B)

        @block.gpsimd
        def _(pool):
            pool.memset(ident[:, :], 0.0).then_inc(ident_set, 1)
            pool.memset(mask_q0[:, :, :], 0.0).then_inc(ident_set, 1)
            pool.memset(mask_k0[:, :, :], 0.0).then_inc(ident_set, 1)
            pool.memset(block_mask[:, :], 1.0).then_inc(ident_set, 1)
            pool.wait_ge(ident_set, 4)
            pool.affine_select(out=ident[:, :], in_=ident[:, :], compare_op=ALU.not_equal, fill=1.0, base=0,
                               pattern=[[-1, P]], channel_multiplier=1).then_inc(ident_set, 1)
            pool.affine_select(out=block_mask[:, :], in_=block_mask[:, :], compare_op=ALU.is_ge, fill=0.0, base=0,
                               pattern=[[-HD, NB]], channel_multiplier=1).then_inc(ident_set, 1)
            pool.wait_ge(ident_set, 6)
            pool.affine_select(out=block_mask[:, :], in_=block_mask[:, :], compare_op=ALU.is_ge, fill=0.0, base=HD - 1,
                               pattern=[[HD, NB]], channel_multiplier=-1).then_inc(ident_set, 1)
            if A.causal:
                pool.affine_select(out=mask_q0[:, :, :], in_=mask_q0[:, :, :], compare_op=ALU.is_ge, fill=-BIG, base=0,
                                   pattern=[[P, NT], [-1, S]], channel_multiplier=1).then_inc(masks_set, 1)
                pool.affine_select(out=mask_k0[:, :, :], in_=mask_k0[:, :, :], compare_op=ALU.is_ge, fill=-BIG, base=0,
                                   pattern=[[-P, NT], [1, S]], channel_multiplier=-1).then_inc(masks_set, 1)
            pool.memset(ones_row[:, :].bitcast(F32), 1.0).then_inc(stacks_set, 1)
            for m in range(2):
                pool.memset(k_stack[m][:, :, :].bitcast(F32), 0.0).then_inc(stacks_set, 1)
            for t in range(NT):
                pool.memset(q_stack[:, t, :, :].bitcast(F32), 0.0).then_inc(stacks_set, 1)
            pool.wait_ge(biases_in, 64)

            def step(i, par):
                if has(i - 1):
                    for t in range(NT):
                        wait(pool, res_loaded[t], 16 * i)
                        pool.tensor_tensor(x_res[:, t, :], x_res[:, t, :], bo[:, :], ALU.add).then_inc(res_biased, 1)

            steps(pool, step)

        @block.scalar
        def _(act):
            for n, (part, st) in enumerate(stages):
                if n < 2:
                    act.wait_ge(w_in[n], 16)
                    act.activation(part[0][:, :, :], st, ACT.Copy).then_inc(w_hi, 1)
            act.wait_ge(biases_in, 64)

            def src_high(n):
                wait(act, src_loaded, 16 * (n + 1))
                wait(act, q_ready, 2 * n)
                act.activation(xt[0][:, :, :], src[:, :, :], ACT.Copy).then_inc(src_hi, 1)

            def t_high(n, t):
                wait(act, t_ready, NT * n + t + 1)
                if cross:
                    wait(act, v_ready, n + 1)
                else:
                    wait(act, q_ready, 2 * n)
                    wait(act, v_ready, n)
                act.activation(xt[0][:, :, t * P:(t + 1) * P], proj[t][:, :].rearrange("p (c q) -> p c q", c=DC), ACT.Copy).then_inc(xt_hi, 1)

            def q_high(n, par, half):
                wait(act, q_ready, 2 * n + half + 1)
                if half == 0:
                    wait(act, q_spilled, Q_ROWS_IN * (n - 1))
                    wait(act, max_ready, NU * (n - 1))
                for c in (2 * half, 2 * half + 1):
                    act.activation(q_parts[par][0][:, c, :], proj[half][:, (c % 2) * S:(c % 2 + 1) * S], ACT.Identity, bias=bq[:, c:c + 1]).then_inc(q_hi, 1)

            def k_high(n):
                wait(act, k_ready, n + 1)
                if cross:
                    wait(act, k_spilled, K_ROWS_IN * n)
                else:
                    wait(act, k_stacked, 16 * 3 * n)
                wait(act, kb_ready, NB * n)
                act.activation(k_parts[0][:, :], proj[0][:, 0:S], ACT.Identity, bias=bk[:, 0:1]).then_inc(k_hi, 1)

            def shift_copy(m, t):
                wait(act, shift_t_ready, NT * m + t + 1)
                wait(act, shift_spilled[t], 16 * m)
                act.activation(shift_t[:, t, :], proj[0][0:NH, 0:P], ACT.Copy).then_inc(shift_t_done, 1)

            def odd_lanes(m, t):
                wait(act, pv_done, NG * m + (A.groups_of_tile0 if t == 0 else NG))
                wait(act, ht_lo, NT * (m - 1) + t + 1)
                wait(act, heads_ready, NT * m + t)
                for h, to in ((1, heads[:, t, :]), (0, recip[:, :])):
                    act.activation(to, odd_ps[:, :], ACT.Copy, scale=lane_half[:, h:h + 1]).then_inc(odd_copied, 1)

            def head_high(m, t):
                wait(act, heads_ready, NT * m + t + 1)
                wait(act, o_ready, NT * (m - 1) + t + 1)
                act.activation(ht[0][:, t, :, :], heads[:, t, :].rearrange("p (c q) -> p c q", c=DC), ACT.Copy).then_inc(ht_hi, 1)

            def step(i, par):
                n, b = i + 1, i - 1
                if isinstance(i, int) and i == 0:
                    act.wait_ge(w_in[2], 16)
                    act.activation(wo[0][:, :, :], stages[2][1], ACT.Copy).then_inc(w_hi, 1)
                if isinstance(i, int) and i == 1:
                    act.wait_ge(w_lo, 3)
                jobs = {
                    "src": (n, lambda: src_high(n)),
                    "t0": (n, lambda: t_high(n, 0)), "t1": (n, lambda: t_high(n, 1)),
                    "q0": (n, lambda: q_high(n, 1 - par, 0)), "q1": (n, lambda: q_high(n, 1 - par, 1)), "k": (n, lambda: k_high(n)),
                    "shift0": (i, lambda: shift_copy(i, 0)), "shift1": (i - 1, lambda: shift_copy(i - 1, 1)),
                    "mix0": (i - 1, lambda: odd_lanes(i - 1, 0)), "mix1": (i - 2, lambda: odd_lanes(i - 2, 1)),
                    "head0": (i - 1, lambda: head_high(i - 1, 0)), "head1": (i - 2, lambda: head_high(i - 2, 1)),
                }
                for u in range(NU):
                    if has(b):
                        k = u // 4
                        half = (NG * (1 - par) + k) % 2
                        if u % 4 == 0:
                            wait(act, pv_done, NG * b + k - 1)
                        wait(act, score_ready, NU * b + u + 1)
                        act.activation(probs[:, half, u % 4, :], score_ps[u % 2][:, :], ACT.Exp, scale=A.scale).then_inc(exp_done, 1)
                    for job in A.act_plan.get(u, ()):
                        m, do = jobs[job]
                        if has(m):
                            do()

            steps(act, step)

        @block.vector
        def _(dve):
            for n, (part, st) in enumerate(stages[:2]):
                dve.wait_ge(w_hi, n + 1)
                dve.tensor_tensor(part[1][:, :, :], st, part[0][:, :, :].bitcast(F32), ALU.subtract).then_inc(w_lo, 1)
            for m in range(2):
                dve.memset(v_use[m][:, :, :, :], 0.0 if A.causal else 1.0).then_inc(consts_set, 1)
            if cross:
                dve.wait_ge(masks_in, 48)
                dve.wait_ge(ident_set, 7)
                dve.tensor_reduce(lane_half[:, :], block_mask[:, :].rearrange("p (j h) -> p h j", h=2), AX.X, ALU.add).then_inc(consts_set, 1)
                dve.tensor_scalar(mask_q0[:, :, :], mask_words[:, 0].bitcast(U8), -BIG, None, ALU.mult).then_inc(consts_set, 1)
                dve.tensor_scalar(mask_k0[:, :, :], mask_words[:, 1].bitcast(U8), -BIG, None, ALU.mult).then_inc(consts_set, 1)
                dve.tensor_scalar(padc_f[:, :], padc_words[:, :].bitcast(U8), -BIG, None, ALU.mult).then_inc(consts_set, 1)
            else:
                dve.memset(ones_v[:, :, :], 1.0).then_inc(consts_set, 1)
            dve.wait_ge(ident_set, 7)
            dve.tensor_copy(ident16[:, :], ident[:, :]).then_inc(consts_set, 1)
            dve.wait_ge(consts_set, (7 if cross else 4))
            dve.wait_ge(biases_in, 64)

            def norm_stats(n):
                wait(dve, x_loaded, 16 * NT * (n + 1))
                for t in range(NT):
                    dve.bn_stats(stats[:, t, :], x_tile[:, t, :]).then_inc(ln_step, 1)

            def norm_root(n):
                wait(dve, ln_step, 16 * n + 2)
                dve.memset(gate[:, 4:5], 0.0)
                for t in range(NT):
                    dve.bn_aggr(mv[:, t, :], stats[:, t, :]).then_inc(ln_step, 1)
                wait(dve, ln_step, 16 * n + 4)
                inverse_root(dve, mv[:, :, 1], (rstd[:, :], square[:, :], half_var[:, :]), ln_step, 16 * n + 4)

            def norm_apply(n):
                wait(dve, ln_step, 16 * n + 16)
                for t in range(NT):
                    dve.tensor_scalar(x_tile[:, t, :], x_tile[:, t, :], mv[:, t, 0:1], rstd[:, t:t + 1], ALU.subtract, ALU.mult).then_inc(xn_ready, 1)

            def src_low(n):
                wait(dve, src_hi, n + 1)
                dve.tensor_tensor(xt[1][:, :, :], src[:, :, :], xt[0][:, :, :].bitcast(F32), ALU.subtract).then_inc(src_lo, 1)

            def t_low(n, t):
                wait(dve, xt_hi, NT * n + t + 1)
                dve.tensor_tensor(xt[1][:, :, t * P:(t + 1) * P], proj[t][:, :].rearrange("p (c q) -> p c q", c=DC),
                                  xt[0][:, :, t * P:(t + 1) * P].bitcast(F32), ALU.subtract).then_inc(xt_lo, 1)

            def q_low(n, par, half):
                wait(dve, q_hi, DC * n + 2 * half + 2)
                for c in (2 * half, 2 * half + 1):
                    dve.scalar_tensor_tensor(out=q_parts[par][1][:, c, :], in0=proj[half][:, (c % 2) * S:(c % 2 + 1) * S], scalar=bq[:, c:c + 1],
                                             in1=q_parts[par][0][:, c, :].bitcast(F32), op0=ALU.add, op1=ALU.subtract).then_inc(q_lo, 1)

            def k_low(n, par):
                wait(dve, k_hi, n + 1)
                dve.scalar_tensor_tensor(out=k_parts[1][:, :], in0=proj[0][:, 0:S], scalar=bk[:, 0:1],
                                         in1=k_parts[0][:, :].bitcast(F32), op0=ALU.add, op1=ALU.subtract).then_inc(k_lo, 1)

            def k_spread(n, par, part):
                wait(dve, k_hi, n + 1)
                wait(dve, max_ready, NU * (n - 1))
                for g in range(part * NB // 2, (part + 1) * NB // 2):
                    dve.tensor_scalar(k_blocks[par][:, g, :], k_parts[0][:, :].bitcast(F32), block_mask[:, g:g + 1], None, ALU.mult).then_inc(kb_ready, 1)

            def v_bias(n):
                wait(dve, v_ready, n + 1)
                wait(dve, v_use_ready, (2 if cross else 1) * n)
                dve.tensor_tensor(v_new[:, :, :], proj[1][:, 0:NT * VD].rearrange("p (t v) -> p t v", t=NT), spread(bv[:, :], NT), ALU.add).then_inc(v_done, 1)

            def query_mask(n, par):
                wait(dve, pad_loaded, 16 * (n + 1))
                dve.tensor_scalar(pad_f[:, :], pad_words[:, :].bitcast(U8), -BIG, None, ALU.mult).then_inc(padf_set, 1)
                wait(dve, padf_set, n + 1)
                wait(dve, max_done, NU * (n - 1))
                dve.tensor_tensor(mask_q[par][:, :, :], mask_q0[:, :, :], spread(pad_f[:, :], NT), ALU.add).then_inc(mask_q_ready, 1)

            def v_and_mask_for_use(m, par):
                wait(dve, pv_done, NG * (m - 1))
                wait(dve, v_done, m + 1)
                if A.causal:
                    dve.tensor_copy(v_use[par][:, :, 0, :], v_new[:, :, :]).then_inc(v_use_ready, 1)
                else:
                    for half in range(2):
                        dve.tensor_copy(v_use[par][:, :, half:NB:2, half * HD:(half + 1) * HD],
                                        v_new[:, :, :].rearrange("p t (j h d) -> p t j h d", h=2, d=HD)[:, :, :, half, :]).then_inc(v_use_ready, 1)
                    wait(dve, score_ready, NU * (m - 1))
                    for kt in range(NT):
                        dve.tensor_scalar(mask_k[par][:, kt, :], mask_k0[:, kt, :], padc_f[:, bass.ds(m * NT + kt, 1)], None, ALU.add).then_inc(mask_k_ready, 1)

            def shifts(m, t):
                wait(dve, max_done, NU * m + (A.max_units_of_tile0 if t == 0 else NU))
                wait(dve, shift_t_ready, NT * (m - 1) + t + 1)
                dve.tensor_scalar(shift[:, t, :].rearrange("p (g c) -> p g c", c=DC), row_max[:, t, :, :], -1.0, SHIFT_MAX,
                                  ALU.mult, ALU.min).then_inc(shift_ready, 1)

            def even_lanes(m, t):
                wait(dve, odd_copied, 2 * (NT * m + t + 1))
                for h, to in ((0, heads[:, t, :]), (1, recip[:, :])):
                    dve.scalar_tensor_tensor(out=to, in0=even_ps[:, :], scalar=lane_half[:, h:h + 1], in1=to, op0=ALU.mult, op1=ALU.add).then_inc(mixed, 1)

            def invert(m, t, part):
                if cross:
                    wait(dve, mixed, 2 * (NT * m + t + 1))
                else:
                    wait(dve, pv_done, NG * m + (A.groups_of_tile0 if t == 0 else NG))
                sums = recip if cross else sums_ps
                dve.reciprocal(recip[:, part * 256:(part + 1) * 256], sums[:, part * 256:(part + 1) * 256]).then_inc(recip_done, 1)

            def normalise(m, t):
                wait(dve, recip_done, 2 * (NT * m + t + 1))
                if cross:
                    dve.memset(gate[:, 5:6], 0.0)
                    dve.stream_shuffle(recip[:, :], recip[:, :], [(lane + HD) % 32 for lane in range(32)]).then_inc(swapped, 1)
                    wait(dve, swapped, NT * m + t + 1)
                    dve.tensor_tensor(heads[:, t, :], heads[:, t, :], recip[:, :], ALU.mult).then_inc(heads_ready, 1)
                else:
                    wait(dve, ht_hi, NT * (m - 1) + t + 1)
                    dve.tensor_tensor(heads[:, t, :], heads_ps[:, :], recip[:, :], ALU.mult).then_inc(heads_ready, 1)

            def head_low(m, t):
                wait(dve, ht_hi, NT * m + t + 1)
                dve.tensor_tensor(ht[1][:, t, :, :].rearrange("p c q -> p (c q)"), heads[:, t, :],
                                  ht[0][:, t, :, :].rearrange("p c q -> p (c q)").bitcast(F32), ALU.subtract).then_inc(ht_lo, 1)

            def out_add(m, t):
                wait(dve, o_ready, NT * m + t + 1)
                wait(dve, res_biased, NT * m + t + 1)
                dve.tensor_tensor(x_res[:, t, :], proj[1][:, :], x_res[:, t, :], ALU.add).then_inc(o_done, 1)

            def step(i, par):
                n = i + 1
                if isinstance(i, int) and i == 0:
                    dve.wait_ge(w_hi, 3)
                    dve.tensor_tensor(wo[1][:, :, :], stages[2][1], wo[0][:, :, :].bitcast(F32), ALU.subtract).then_inc(w_lo, 1)
                jobs = {
                    "stats": (n, lambda: norm_stats(n)), "root": (n, lambda: norm_root(n)), "apply": (n, lambda: norm_apply(n)), "src": (n, lambda: src_low(n)),
                    "t0": (n, lambda: t_low(n, 0)), "t1": (n, lambda: t_low(n, 1)),
                    "q0": (n, lambda: q_low(n, 1 - par, 0)), "q1": (n, lambda: q_low(n, 1 - par, 1)),
                    "k": (n, lambda: k_low(n, 1 - par)),
                    "kb0": (n, lambda: k_spread(n, 1 - par, 0)), "kb1": (n, lambda: k_spread(n, 1 - par, 1)), "v": (n, lambda: v_bias(n)), "mask": (n, lambda: query_mask(n, 1 - par)),
                    "v_use": (i, lambda: v_and_mask_for_use(i, par)),
                    "mix0": (i - 1, lambda: even_lanes(i - 1, 0)), "mix1": (i - 2, lambda: even_lanes(i - 2, 1)),
                    "inv00": (i - 1, lambda: invert(i - 1, 0, 0)), "inv01": (i - 1, lambda: invert(i - 1, 0, 1)), "norm0": (i - 1, lambda: normalise(i - 1, 0)),
                    "inv10": (i - 2, lambda: invert(i - 2, 1, 0)), "inv11": (i - 2, lambda: invert(i - 2, 1, 1)), "norm1": (i - 2, lambda: normalise(i - 2, 1)),
                    "head0": (i - 1, lambda: head_low(i - 1, 0)), "head1": (i - 2, lambda: head_low(i - 2, 1)),
                    "out0": (i - 1, lambda: out_add(i - 1, 0)), "out1": (i - 2, lambda: out_add(i - 2, 1)),
                }
                for u, (qt, c, blk, nb, width) in enumerate(A.max_units):
                    if has(i):
                        if cross and u == 0:
                            wait(dve, mask_q_ready, i + 1)
                        wait(dve, max_ready, NU * i + u + 1)
                        if cross:
                            dve.memset(gate[:, u % 4:u % 4 + 1], 0.0)
                            for j in range(nb):
                                scores = max_ps[u % 2][:, j * width:(j + 1) * width]
                                mx = dve.tensor_tensor_reduce(scores, scores, mask_q[par][:, qt, :], 1.0, -FLOOR,
                                                              ALU.add, ALU.max, row_max[:, qt, blk + j, c:c + 1])
                            mx.then_inc(max_done, 1)
                        else:
                            dve.tensor_reduce(row_max[:, qt, blk:blk + nb, c], max_ps[u % 2][:, :].rearrange("p (b k) -> p b k", b=nb),
                                              AX.X, ALU.max).then_inc(max_done, 1)
                        if u == A.max_units_of_tile0 - 1:
                            shifts(i, 0)
                        if u == NU - 1:
                            shifts(i, 1)
                    for job in A.dve_plan.get(u, ()):
                        m, do = jobs[job]
                        if has(m):
                            do()

            steps(dve, step)

        @block.tensor
        def _(pe):
            pe.wait_ge(consts_set, (7 if cross else 4))
            if A.causal:
                pe.wait_ge(masks_set, 2)
            pe.wait_ge(w_lo, 2)

            def three(out, a, b, first, last):
                for k, (x, y) in enumerate(((0, 0), (1, 0), (0, 1))):
                    mm = pe.matmul(out, a[x], b[y], start=first and k == 0, stop=last and k == 2)
                return mm

            def max_unit(i, par, u):
                qt, c, blk, nb, width = A.max_units[u]
                if u == 0:
                    wait(pe, kb_ready, NB * (i + 1))
                    wait(pe, q_hi, DC * (i + 1))
                wait(pe, max_done, NU * i + u - 1)
                out = max_ps[u % 2][:, :]
                mm = pe.matmul(out, q_parts[par][0][:, c, qt * P:(qt + 1) * P], k_blocks[par][:, blk:blk + nb, 0:width], start=True, stop=cross)
                if A.causal:
                    diagonal = out.rearrange("p (b k) -> p b k", b=nb)[:, :, qt * P:(qt + 1) * P]
                    mm = pe.matmul(diagonal, ident16[:, :], spread(mask_q0[:, qt, qt * P:(qt + 1) * P], nb), start=False, stop=True)
                mm.then_inc(max_ready, 1)

            def score_unit(b, par, u):
                qt, half, blocks, kt, first, last = A.groups[u // 4]
                g = blocks[u % 4]
                masked = cross or kt == qt
                if u == 0:
                    wait(pe, k_stacked, 16 * 3 * (b + 1))
                    if cross:
                        wait(pe, mask_k_ready, NT * (b + 1))
                if u == 4 * A.groups_of_tile0 * qt:
                    wait(pe, q_stacked[qt], 16 * 3 * (b + 1))
                    wait(pe, shift_stacked[qt], 16 * (b + 1))
                wait(pe, exp_done, NU * b + u - 1)
                out = score_ps[u % 2][:, :]
                mm = pe.matmul(out, k_stack[par][:, 0 if A.causal else g, kt * P:(kt + 1) * P],
                               q_stack[:, qt, g * DC:(g + 1) * DC, :], start=True, stop=not masked)
                if masked:
                    mm = pe.matmul(out, ident16[:, :], spread(mask_k[par][:, kt, qt * P:(qt + 1) * P], DC), start=False, stop=True)
                mm.then_inc(score_ready, 1)

            def pv_group(b, par, k):
                qt, half, blocks, kt, first, last = A.groups[k]
                wait(pe, exp_done, NU * b + 4 * (k + 1))
                if k == 0:
                    wait(pe, v_use_ready, (2 if cross else 1) * (b + 1))
                if first and cross:
                    wait(pe, mixed, 2 * (NT * b + qt))
                elif first:
                    wait(pe, heads_ready, NT * b + qt)
                if cross:
                    products = ((even_ps, odd_ps)[half], lambda g: v_use[par][:, kt, g, :]),
                    first, last = kt == 0, kt == NT - 1
                else:
                    products = (heads_ps, lambda g: v_use[par][:, kt, 0, :]), (sums_ps, lambda g: ones_v[:, half, :])
                for out_ps, w_of in products:
                    for j, g in enumerate(blocks):
                        mm = pe.matmul(out_ps[32 * j:32 * j + 32, :], w_of(g), probs[:, (NG * par + k) % 2, j, :],
                                       start=first, stop=last, tile_position=(0, 32 * j))
                mm.then_inc(pv_done, 1)

            def shift_turn(i, t):
                if t == 1:
                    wait(pe, shift_t_done, NT * i + 1)
                elif has(i + 1):
                    wait(pe, q_lo, DC * (i + 1) + 2)
                else:
                    wait(pe, shift_t_done, NT * i)
                wait(pe, shift_ready, NT * i + t + 1)
                pe.transpose(proj[0][0:NH, 0:P], shift[:, t, :], ident[:, :]).then_inc(shift_t_ready, 1)

            def out_project(m, t):
                if t == 1:
                    wait(pe, o_done, NT * m + 1)
                elif has(m + 2):
                    wait(pe, q_lo, DC * (m + 2) + 4)
                else:
                    wait(pe, o_done, NT * m)
                wait(pe, ht_lo, NT * m + t + 1)
                for c in range(DC):
                    mm = three(proj[1][:, :], [h[:, t, c, :] for h in ht], [h[:, c, :] for h in wo], c == 0, c == DC - 1)
                mm.then_inc(o_ready, 1)

            def first_in_proj0(n):
                if has(n - 2):
                    wait(pe, shift_t_done, NT * (n - 1))
                elif has(n - 1):
                    wait(pe, q_lo, DC * (n - 1) + 2)

            def first_in_proj1(n):
                if has(n - 3):
                    wait(pe, o_done, NT * (n - 2))
                elif has(n - 1):
                    wait(pe, q_lo, DC * n)

            def turn(n, t):
                if cross:
                    wait(pe, (k_lo, v_done)[t], n + 1)
                else:
                    (first_in_proj0, first_in_proj1)[t](n)
                wait(pe, xn_ready, NT * n + t + 1)
                for c in range(DC):
                    mm = pe.transpose(proj[t][:, c * P:(c + 1) * P], x_tile[:, t, c * P:(c + 1) * P], ident[:, :])
                mm.then_inc(t_ready, 1)

            def q_project(n, half):
                wait(pe, xt_lo, NT * (n + 1))
                if not cross:
                    wait(pe, (k_lo, v_done)[half], n + 1)
                for c in (2 * half, 2 * half + 1):
                    for k in range(DC):
                        mm = three(proj[half][:, (c % 2) * S:(c % 2 + 1) * S], [h[:, k, c * P:(c + 1) * P] for h in wq],
                                   [h[:, k, :] for h in xt], k == 0, k == DC - 1)
                mm.then_inc(q_ready, 1)

            def k_project(n):
                if cross:
                    first_in_proj0(n)
                    wait(pe, src_lo, n + 1)
                else:
                    wait(pe, xt_lo, NT * (n + 1))
                for k in range(DC):
                    mm = three(proj[0][:, 0:S], [h[:, k, 0:P] for h in wkv], [h[:, k, :] for h in xt], k == 0, k == DC - 1)
                mm.then_inc(k_ready, 1)

            def v_project(n):
                if cross:
                    first_in_proj1(n)
                    wait(pe, src_lo, n + 1)
                else:
                    wait(pe, xt_lo, NT * (n + 1))
                for t in range(NT):
                    for k in range(DC):
                        mm = three(proj[1][:, t * VD:(t + 1) * VD], [h[:, k, t * P:(t + 1) * P] for h in xt],
                                   [h[:, k, P:P + VD] for h in wkv], k == 0, k == DC - 1)
                mm.then_inc(v_ready, 1)

            def step(i, par):
                n, b = i + 1, i - 1
                if isinstance(i, int) and i == 1:
                    pe.wait_ge(w_lo, 3)
                jobs = {
                    "t0": (n, lambda: turn(n, 0)), "t1": (n, lambda: turn(n, 1)), "k": (n, lambda: k_project(n)), "v": (n, lambda: v_project(n)),
                    "q0": (n, lambda: q_project(n, 0)), "q1": (n, lambda: q_project(n, 1)),
                    "shift0": (i, lambda: shift_turn(i, 0)), "shift1": (i - 1, lambda: shift_turn(i - 1, 1)),
                    "out0": (i - 1, lambda: out_project(i - 1, 0)), "out1": (i - 2, lambda: out_project(i - 2, 1)),
                }
                for u in range(NU):
                    if has(b):
                        score_unit(b, 1 - par, u)
                    if has(i):
                        max_unit(i, par, u)
                    if u == 1 and has(i - 2):
                        pv_group(i - 2, par, NG - 1)
                    if u % 4 == 1 and u > 4 and has(b):
                        pv_group(b, 1 - par, u // 4 - 1)
                    for job in A.pe_plan.get(u, ()):
                        m, do = jobs[job]
                        if has(m):
                            do()

            steps(pe, step)


def build_ffn(nc, B, x_in, x_out, w0, b0, w1, b1):
    F = w0.shape[1]
    FC = F // P
    TOK = 512
    TT = TOK // P
    N = B * S // TOK
    RING = 4
    LAG = 2
    LN = 2 * TT + 12
    with ExitStack() as es:
        def sb(name, shape, dt):
            return es.enter_context(nc.sbuf_tensor(f"ffn_{name}", shape, dt))

        def pb(name, shape, dt=F32):
            return es.enter_context(nc.psum_tensor(f"ffn_{name}", shape, dt))

        def sem(name):
            return es.enter_context(nc.semaphore(f"ffn_{name}"))

        stage = sb("stage", [P, 2, 4, 512], F32)
        w0s = [sb(f"w0{n}", [P, DC, F], F32R) for n in range(2)]
        w1s = [sb(f"w1{n}", [P, FC, D], F32R) for n in range(2)]
        bias0 = sb("bias0", [P, FC], F32)
        bias1 = sb("bias1", [P, D], F32)
        ident = sb("ident", [P, P], F32)
        ident16 = sb("ident16", [P, P], F16)
        x_tile = sb("x_tile", [P, TT, D], F32)
        x_res = sb("x_res", [P, TT, D], F32)
        stats = sb("stats", [P, TT, 6], F32)
        mv = sb("mv", [P, TT, 2], F32)
        square = sb("square", [P, TT], F32)
        half_var = sb("half_var", [P, TT], F32)
        rstd = sb("rstd", [P, TT], F32)
        gate = sb("gate", [P, 1], F32)
        xn = sb("xn", [P, TT, D], F16)
        xt = [sb(f"xt{m}", [P, DC, TOK], F32R) for m in range(2)]
        h16 = sb("h16", [P, 2, TOK], F16)
        hid = sb("hid", [P, RING, TOK], F32R)
        e16 = sb("e16", [P, TT, D], F16)

        turn_ps = pb("turn_ps", [P, 2, 2 * D], F16)
        up_ps = [pb(f"up{n}", [P, TOK]) for n in range(2)]
        down_ps = [pb(f"down{n}", [P, D]) for n in range(TT)]

        biases_in, w_in, w_hi, w_lo = sem("biases_in"), [sem("w_in0"), sem("w_in1")], sem("w_hi"), sem("w_lo")
        ident_set, ident16_set = sem("ident_set"), sem("ident16_set")
        x_loaded, res_loaded, ln_step, xn_ready = sem("x_loaded"), sem("res_loaded"), sem("ln_step"), sem("xn_ready")
        t_ready, xt_ready = sem("t_ready"), sem("xt_ready")
        up_ready, gelu_done, hid_ready, used = sem("up_ready"), sem("gelu_done"), sem("hid_ready"), sem("used")
        e_ready, out_ready, stored = sem("e_ready"), sem("out_ready"), sem("stored")
        block = es.enter_context(nc.Block())

        def rows(dram, i):
            v = dram.rearrange("b s d -> (b s) d").rearrange("(n t p) d -> n p t d", t=TT, p=P)
            return v[bass.ds(i, 1), :, :, :].rearrange("a p t d -> (a p) t d")

        pieces = []
        for q in range(FC // 4):
            cols = slice(q * 512, (q + 1) * 512)
            pieces.append((w0[:, cols].rearrange("(c p) n -> p c n", p=P), [h[:, :, cols] for h in w0s]))
            pieces.append((w1[cols, :].rearrange("(c p) n -> p c n", p=P), [h[:, 4 * q:4 * q + 4, :] for h in w1s]))
        split_after = {3: (2, 3), 7: (4, 5), 11: (6, 7)}

        def steps(engine, step):
            step(0, 0)
            with engine.Fori(1, N - 2, 2) as i:
                step(i, 1)
                step(i + 1, 0)
            step(N - 1, 1)

        def more(i):
            return not isinstance(i, int) or i + 1 < N

        @block.sync
        def _(sp):
            sp.dma_start(x_tile[:, :, :], rows(x_in, 0)).then_inc(x_loaded, 16)
            sp.dma_start(bias0[:, :], b0).then_inc(biases_in, 16)
            sp.dma_start(bias1[:, :], b1.partition_broadcast(P)).then_inc(biases_in, 16)
            for n, (src, _) in enumerate(pieces):
                if n == 4:
                    sp.wait_ge(xn_ready, TT)
                    sp.dma_start(x_tile[:, :, :], rows(x_in, 1)).then_inc(x_loaded, 16)
                wait(sp, w_lo, n - 1)
                sp.dma_start(stage[:, n % 2], src).then_inc(w_in[n % 2], 16)

            def step(i, par):
                if more(i) and not (isinstance(i, int) and i == 0):
                    wait(sp, xn_ready, TT * (i + 1))
                    sp.dma_start(x_tile[:, :, :], rows(x_in, i + 1)).then_inc(x_loaded, 16)
                wait(sp, stored, 16 * i)
                sp.dma_start(x_res[:, :, :], rows(x_in, i)).then_inc(res_loaded, 16)
                wait(sp, out_ready, TT * (i + 1))
                sp.dma_start(rows(x_out, i), x_res[:, :, :]).then_inc(stored, 16)

            steps(sp, step)
            sp.wait_ge(stored, 16 * N)

        @block.gpsimd
        def _(pool):
            pool.memset(ident[:, :], 0.0).then_inc(ident_set, 1)
            pool.wait_ge(ident_set, 1)
            pool.affine_select(out=ident[:, :], in_=ident[:, :], compare_op=ALU.not_equal, fill=1.0, base=0,
                               pattern=[[-1, P]], channel_multiplier=1).then_inc(ident_set, 1)

            def step(i, par):
                wait(pool, res_loaded, 16 * (i + 1))
                for t in range(TT):
                    wait(pool, e_ready, TT * i + t + 1)
                    pool.tensor_tensor(x_res[:, t, :], x_res[:, t, :], e16[:, t, :], ALU.add).then_inc(out_ready, 1)

            steps(pool, step)

        @block.scalar
        def _(act):
            def split(n):
                act.wait_ge(w_in[n % 2], 16 * (n // 2 + 1))
                act.activation(pieces[n][1][0], stage[:, n % 2], ACT.Copy).then_inc(w_hi, 1)

            def turned(n, par, t):
                wait(act, t_ready, TT * n + t + 1)
                act.activation(xt[par][:, :, t * P:(t + 1) * P], turn_ps[:, t % 2, 0:D].rearrange("p (c q) -> p c q", c=DC), ACT.Copy).then_inc(xt_ready, 1)

            split(0)
            for t in range(TT):
                turned(0, 0, t)
            split(1)
            act.wait_ge(biases_in, 32)

            def step(i, par):
                for f in range(FC):
                    wait(act, up_ready, FC * i + f + 1)
                    wait(act, hid_ready, FC * i + f - 1)
                    act.activation(h16[:, f % 2, :], up_ps[f % 2][:, :], ACT.Gelu, bias=bias0[:, f:f + 1]).then_inc(gelu_done, 1)
                    if isinstance(i, int) and i == 0:
                        for n in split_after.get(f, ()):
                            split(n)
                    if more(i) and 9 <= f < 9 + TT:
                        turned(i + 1, 1 - par, f - 9)

            steps(act, step)

        @block.vector
        def _(dve):
            def split(n):
                dve.wait_ge(w_hi, n + 1)
                dve.tensor_tensor(pieces[n][1][1], stage[:, n % 2], pieces[n][1][0].bitcast(F32), ALU.subtract).then_inc(w_lo, 1)

            def norm_stats(n, t):
                if t == 0:
                    wait(dve, x_loaded, 16 * (n + 1))
                dve.bn_stats(stats[:, t, :], x_tile[:, t, :]).then_inc(ln_step, 1)

            def norm_root(n):
                wait(dve, ln_step, LN * n + TT)
                dve.memset(gate[:, :], 0.0)
                for t in range(TT):
                    dve.bn_aggr(mv[:, t, :], stats[:, t, :]).then_inc(ln_step, 1)
                wait(dve, ln_step, LN * n + 2 * TT)
                inverse_root(dve, mv[:, :, 1], (rstd[:, :], square[:, :], half_var[:, :]), ln_step, LN * n + 2 * TT)

            def norm_apply(n):
                wait(dve, ln_step, LN * (n + 1))
                wait(dve, t_ready, TT * n)
                for t in range(TT):
                    dve.tensor_scalar(xn[:, t, :], x_tile[:, t, :], mv[:, t, 0:1], rstd[:, t:t + 1], ALU.subtract, ALU.mult).then_inc(xn_ready, 1)

            dve.wait_ge(ident_set, 2)
            dve.tensor_copy(ident16[:, :], ident[:, :]).then_inc(ident16_set, 1)
            for t in range(TT):
                norm_stats(0, t)
            norm_root(0)
            norm_apply(0)
            split(0)
            split(1)
            dve.wait_ge(biases_in, 32)

            def step(i, par):
                for f in range(FC):
                    wait(dve, gelu_done, FC * i + f + 1)
                    wait(dve, used, FC * i + f - RING + 1)
                    dve.tensor_copy(hid[:, f % RING, :], h16[:, f % 2, :]).then_inc(hid_ready, 1)
                    if isinstance(i, int) and i == 0:
                        for n in split_after.get(f, ()):
                            split(n)
                    if more(i):
                        if 1 <= f < 1 + TT:
                            norm_stats(i + 1, f - 1)
                        if f == 5:
                            norm_root(i + 1)
                        if f == 6:
                            norm_apply(i + 1)
                wait(dve, out_ready, TT * i)
                wait(dve, used, FC * (i + 1))
                for t in range(TT):
                    dve.tensor_tensor(e16[:, t, :], down_ps[t][:, :], bias1[:, :], ALU.add).then_inc(e_ready, 1)

            steps(dve, step)

        @block.tensor
        def _(pe):
            def turn(n, t):
                wait(pe, xn_ready, TT * n + t + 1)
                wait(pe, xt_ready, TT * n + t - 1)
                for c in range(DC):
                    mm = pe.transpose(turn_ps[:, t % 2, c * P:(c + 1) * P], xn[:, t, c * P:(c + 1) * P], ident16[:, :])
                mm.then_inc(t_ready, 1)

            pe.wait_ge(ident16_set, 1)
            for t in range(TT):
                turn(0, t)

            def step(i, par):
                wait(pe, xt_ready, TT * (i + 1))
                for f in range(FC + LAG):
                    if f < FC:
                        if isinstance(i, int) and i == 0 and f % 4 == 0:
                            pe.wait_ge(w_lo, f // 2 + 1)
                        wait(pe, gelu_done, FC * i + f - 1)
                        for k in range(DC):
                            for h in range(2):
                                mm = pe.matmul(up_ps[f % 2][:, :], w0s[h][:, k, f * P:(f + 1) * P], xt[par][:, k, :],
                                               start=(k == 0 and h == 0), stop=(k == DC - 1 and h == 1))
                        mm.then_inc(up_ready, 1)
                    g = f - LAG
                    if g >= 0:
                        if isinstance(i, int) and i == 0 and g % 4 == 0:
                            pe.wait_ge(w_lo, g // 2 + 2)
                        wait(pe, hid_ready, FC * i + g + 1)
                        if g == 0:
                            wait(pe, e_ready, TT * i)
                        for t in range(TT):
                            for h in range(2):
                                mm = pe.matmul(down_ps[t][:, :], hid[:, g % RING, t * P:(t + 1) * P], w1s[h][:, g, :],
                                               start=(g == 0 and h == 0), stop=(g == FC - 1 and h == 1))
                        mm.then_inc(used, 1)
                    if more(i) and 8 <= f < 8 + TT:
                        turn(i + 1, f - 8)

            steps(pe, step)


def build(nc, a, out):
    B = a["x"].shape[0]
    x1 = nc.dram_tensor("x_after_self", a["x"].shape, F32, kind="Internal").ap()
    x2 = nc.dram_tensor("x_after_cross", a["x"].shape, F32, kind="Internal").ap()
    build_attention(nc, Attention("self", 32, True), B, a["x"], x1,
                    dict(q=a["self_wq"], kv=a["self_wkv"], o=a["self_wo"], bq=a["self_bq"], bk=a["self_bk"], bv=a["self_bv"], bo=a["self_bo"]))
    build_attention(nc, Attention("cross", 16, False), B, x1, x2,
                    dict(q=a["cross_wq"], kv=a["cross_wkv"], o=a["cross_wo"], bq=a["cross_bq"], bk=a["cross_bk"], bv=a["cross_bv"], bo=a["cross_bo"]),
                    ctx_t=a["ctx_t"], mask=a["mask"], mask_t=a["mask_t"], pad=a["pad"], pad_col=a["pad_col"])
    build_ffn(nc, B, x2, out, a["w0"], a["b0"], a["w1"], a["b1"])


def kernel(**inputs):
    import numpy as np
    import concourse.bacc as bacc
    from concourse.bass_utils import run_bass_kernel_spmd

    i = {k: np.asarray(v) for k, v in inputs.items()}
    order = np.arange(512).reshape(8, 4, 16).transpose(1, 0, 2).reshape(512)
    wqkv, bqkv = i["L0_attn_Wqkv_w"], i["L0_attn_Wqkv_b"]
    lay = {
        "x": i["x"],
        "self_wq": wqkv[:512].T, "self_wkv": np.concatenate([np.tile(wqkv[512:544].T, (1, 4)), wqkv[544:].T], 1),
        "self_wo": i["L0_attn_out_w"].T,
        "self_bq": bqkv[:512].reshape(4, 128).T, "self_bk": np.tile(bqkv[512:544], 4).reshape(128, 1),
        "self_bv": bqkv[544:], "self_bo": i["L0_attn_out_b"],
        "cross_wq": i["L0_xattn_Wq"].T[:, order], "cross_wkv": np.concatenate([i["L0_xattn_Wk"].T, i["L0_xattn_Wv"].T], 1),
        "cross_wo": i["L0_xattn_Wo"].T[order],
        "cross_bq": i["L0_xattn_bq"][order].reshape(4, 128).T, "cross_bk": i["L0_xattn_bk"].reshape(128, 1),
        "cross_bv": i["L0_xattn_bv"], "cross_bo": i["L0_xattn_bo"],
        "ctx_t": i["ctx_2048"].transpose(0, 2, 1),
        "mask": i["mask_SxS2_bc0"].view(np.uint32), "mask_t": np.ascontiguousarray(i["mask_SxS2_bc0"].T).view(np.uint32),
        "pad": i["mask_BxS2_bk0"].view(np.uint32),
        "pad_col": np.ascontiguousarray(i["mask_BxS2_bk0"].reshape(32, 128).T).view(np.uint32),
        "w0": i["L0_ffn_W0"].T, "b0": i["L0_ffn_bias0"].reshape(16, 128).T,
        "w1": i["L0_ffn_W1"].T, "b1": i["L0_ffn_bias1"],
    }
    nc = bacc.Bacc("TRN2", target_bir_lowering=False, num_devices=1)
    arrays, aps = {}, {}
    for name, v in lay.items():
        v = np.ascontiguousarray(v)
        arrays[f"in_{name}"] = v
        aps[name] = nc.dram_tensor(f"in_{name}", v.shape, mybir.dt.from_np(v.dtype), kind="ExternalInput").ap()
    out = nc.dram_tensor("out_x", i["x"].shape, F32, kind="ExternalOutput").ap()
    build(nc, aps, out)
    r = run_bass_kernel_spmd(nc, [arrays], core_ids=[0])
    return r.results[0]["out_x"]
```
